# Optimizing a Trainium2 kernel written in Bass

```python
import numpy as np
import jax
import jax.numpy as jnp

def _softmax(x, axis=-1):
    return jax.nn.softmax(x, axis=axis)

def _gelu(x):
    return jax.nn.gelu(x, approximate=True)

def _silu(x):
    return jax.nn.silu(x)

def _sigmoid(x):
    return jax.nn.sigmoid(x)

def _layernorm(x, axis=-1, eps=1e-05):
    m = jnp.mean(x, axis=axis, keepdims=True)
    v = jnp.var(x, axis=axis, keepdims=True)
    return (x - m) / jnp.sqrt(v + eps)

def _scatter_add(tgt, idx, src, axis=0):
    return tgt.at[idx].add(src)

def _segment_sum(src, seg, n):
    return jax.ops.segment_sum(src, seg, n)
kernel_name = 'mk_adaln_ffn_d2_seqx_r8_e9e77b'

def setup_inputs(seed: int=0):
    np.random.seed(seed)
    _w = jnp.asarray

    def _rec_inputs():
        import jax
        import jax.numpy as jnp
        _rk = jax.random.key(seed)
        x = -0.0003929 + 0.9999 * jax.random.normal(jax.random.fold_in(_rk, 1), (64, 32, 512), jnp.float32)
        _lenS = 32 - jax.random.randint(jax.random.fold_in(_rk, 7), (64,), 0, max(1, 32 // 4) + 1, jnp.int32)
        _lenS2 = 32 - jax.random.randint(jax.random.fold_in(_rk, 8), (64,), 0, max(1, 32 // 4) + 1, jnp.int32)
        itok_B_8_3872 = jax.random.randint(jax.random.fold_in(_rk, 11), (64,), 8, 3873, jnp.int32)
        itok_Bx16_0_63 = jax.random.randint(jax.random.fold_in(_rk, 12), (64, 16), 0, 64, jnp.int32)
        itok_B_207_1644 = jax.random.randint(jax.random.fold_in(_rk, 13), (64,), 207, 1645, jnp.int32)
        return (x, itok_B_8_3872, itok_Bx16_0_63, itok_B_207_1644)
    x, itok_B_8_3872, itok_Bx16_0_63, itok_B_207_1644 = _rec_inputs()

    def _L0_cond_setup():
        import math
        import jax, jax.numpy as jnp
        import numpy as np
        H, N, B, L = (32, 64, 16, 512)
        DT_MIN, DT_MAX = (0.001, 0.1)

        def _get_kernel(log_dt, C, log_A_real, A_imag, length):
            Cc = C[..., 0] + 1j * C[..., 1]
            dt = jnp.exp(log_dt)
            A = -jnp.exp(log_A_real) + 1j * A_imag
            dtA = A * dt[:, None]
            P = dtA[:, :, None] * jnp.arange(length, dtype=jnp.float32)
            Cs = Cc * (jnp.exp(dtA) - 1.0) / A
            K = 2.0 * jnp.einsum('hn,hnl->hl', Cs, jnp.exp(P)).real
            return K
        key = jax.random.key(seed)
        ks = jax.random.split(key, 6)
        u = jax.random.normal(ks[0], (B, H, L), dtype=jnp.float32)
        length = jax.random.randint(ks[1], (B,), 0, L)
        log_dt = jax.random.uniform(ks[2], (H,), dtype=jnp.float32) * (math.log(DT_MAX) - math.log(DT_MIN)) + math.log(DT_MIN)
        C = jax.random.normal(ks[3], (H, N, 2), dtype=jnp.float32)
        log_A_real = jnp.log(0.5 * jnp.ones((H, N), dtype=jnp.float32))
        A_imag = math.pi * jnp.broadcast_to(jnp.arange(N, dtype=jnp.float32), (H, N))
        D = jax.random.normal(ks[4], (H,), dtype=jnp.float32)
        return {'u': u, 'length': length, 'log_dt': log_dt, 'C': C, 'log_A_real': log_A_real, 'A_imag': A_imag, 'D': D}
    _L0_cond_all = _L0_cond_setup()
    _L0_cond_in = {k: v for k, v in _L0_cond_all.items() if k in ('log_dt', 'C', 'log_A_real', 'A_imag', 'D')}
    del _L0_cond_all

    def _L0_ffn_setup():
        import jax, jax.numpy as jnp
        import numpy as np
        BATCH, TOK, DIM, OUT = (4, 256, 512, 512)
        E, R, TOP_K = (8, 16, 2)
        SCALING = 16.0 / R
        key = jax.random.key(seed)
        ks = jax.random.split(key, 6)
        return {'x': jax.random.normal(ks[0], (BATCH, TOK, DIM), dtype=jnp.float32), 'W_base': jax.random.normal(ks[1], (OUT, DIM), dtype=jnp.float32) / np.sqrt(DIM), 'b_base': jax.random.normal(ks[2], (OUT,), dtype=jnp.float32) * 0.01, 'W_gate': jax.random.normal(ks[3], (E, DIM), dtype=jnp.float32) * 0.01, 'A': jax.random.normal(ks[4], (E, R, DIM), dtype=jnp.float32) / np.sqrt(DIM), 'B': jax.random.normal(ks[5], (OUT, OUT // OUT * R * 0 + R), dtype=jnp.float32)[None].repeat(E, 0) * 0.0 + jax.random.normal(ks[5], (E, OUT, R), dtype=jnp.float32) * 0.02}
    _L0_ffn_all = _L0_ffn_setup()
    _L0_ffn_in = {k: v for k, v in _L0_ffn_all.items() if k in ('W_base', 'b_base', 'W_gate', 'A', 'B')}
    del _L0_ffn_all

    def _L1_cond_setup():
        import jax, jax.numpy as jnp
        import numpy as np
        B, S, HID = (4, 128, 512)
        D, HQ, HK = (128, 32, 8)
        PAGES, PSIZE, NPP = (64, 32, 16)
        THETA = 10000.0
        EPS = 1e-06
        SCALE = 1.0 / float(np.sqrt(D))

        def _rmsnorm(t, w):
            var = jnp.mean(t * t, axis=-1, keepdims=True)
            return t * jax.lax.rsqrt(var + EPS) * w

        def _rope(t, pos):
            inv_freq = 1.0 / THETA ** (jnp.arange(0, D, 2, dtype=jnp.float32) / D)
            freqs = pos[..., None].astype(jnp.float32) * inv_freq
            cos = jnp.cos(freqs)[:, :, None, :]
            sin = jnp.sin(freqs)[:, :, None, :]
            t1, t2 = (t[..., :D // 2], t[..., D // 2:])
            return jnp.concatenate([t1 * cos - t2 * sin, t2 * cos + t1 * sin], axis=-1)
        key = jax.random.key(seed)
        ks = jax.random.split(key, 10)
        x = jax.random.normal(ks[0], (B, S, HID), jnp.float32)
        Wq = jax.random.normal(ks[1], (HQ * D, HID), jnp.float32) * 0.02
        Wk = jax.random.normal(ks[2], (HK * D, HID), jnp.float32) * 0.02
        Wv = jax.random.normal(ks[3], (HK * D, HID), jnp.float32) * 0.02
        Wo = jax.random.normal(ks[4], (HID, HQ * D), jnp.float32) * 0.02
        q_norm_w = jax.random.uniform(ks[5], (D,), jnp.float32)
        k_norm_w = jax.random.uniform(ks[6], (D,), jnp.float32)
        k_cache = jax.random.normal(ks[7], (PAGES, PSIZE, HK, D), jnp.float32)
        v_cache = jax.random.normal(ks[8], (PAGES, PSIZE, HK, D), jnp.float32)
        block_table = jnp.arange(B * NPP, dtype=jnp.int32).reshape(B, NPP)
        cache_seqlens = jax.random.randint(ks[9], (B,), 0, 475).astype(jnp.int32)
        return dict(x=x, Wq=Wq, Wk=Wk, Wv=Wv, Wo=Wo, q_norm_w=q_norm_w, k_norm_w=k_norm_w, k_cache=k_cache, v_cache=v_cache, block_table=block_table, cache_seqlens=cache_seqlens)
    _L1_cond_all = _L1_cond_setup()
    _L1_cond_in = {k: v for k, v in _L1_cond_all.items() if k in ('Wq', 'Wk', 'Wv', 'Wo', 'q_norm_w', 'k_norm_w', 'k_cache', 'v_cache')}
    del _L1_cond_all

    def _L1_ffn_setup():
        import jax, jax.numpy as jnp
        import numpy as np
        D_IN = 512
        D_OUT = 512
        RANK = 16
        NUM_EXPERTS = 8
        TOP_K = 2
        SCALING = 32.0 / RANK
        key = jax.random.key(seed)
        ks = jax.random.split(key, 6)
        x = jax.random.normal(ks[0], (4, 256, D_IN), dtype=jnp.float32)
        W_base = jax.random.normal(ks[1], (D_OUT, D_IN), dtype=jnp.float32) * (1.0 / np.sqrt(D_IN))
        b_base = jax.random.normal(ks[2], (D_OUT,), dtype=jnp.float32) * 0.01
        W_router = jax.random.normal(ks[3], (NUM_EXPERTS, D_IN), dtype=jnp.float32) * 0.01
        A_stack = jax.random.uniform(ks[4], (NUM_EXPERTS, RANK, D_IN), dtype=jnp.float32, minval=-1.0, maxval=1.0) * (1.0 / np.sqrt(D_IN))
        B_stack = jax.random.normal(ks[5], (NUM_EXPERTS, D_OUT, RANK), dtype=jnp.float32) * 0.02
        return {'x': x, 'W_base': W_base, 'b_base': b_base, 'W_router': W_router, 'A_stack': A_stack, 'B_stack': B_stack}
    _L1_ffn_all = _L1_ffn_setup()
    _L1_ffn_in = {k: v for k, v in _L1_ffn_all.items() if k in ('W_base', 'b_base', 'W_router', 'A_stack', 'B_stack')}
    del _L1_ffn_all
    return {'x': x, 'itok_B_8_3872': itok_B_8_3872, 'itok_Bx16_0_63': itok_Bx16_0_63, 'itok_B_207_1644': itok_B_207_1644, 'L0_cond_log_dt': _L0_cond_in['log_dt'], 'L0_cond_C': _L0_cond_in['C'], 'L0_cond_log_A_real': _L0_cond_in['log_A_real'], 'L0_cond_A_imag': _L0_cond_in['A_imag'], 'L0_cond_D': _L0_cond_in['D'], 'L0_ffn_W_base': _L0_ffn_in['W_base'], 'L0_ffn_b_base': _L0_ffn_in['b_base'], 'L0_ffn_W_gate': _L0_ffn_in['W_gate'], 'L0_ffn_A': _L0_ffn_in['A'], 'L0_ffn_B': _L0_ffn_in['B'], 'L1_cond_Wq': _L1_cond_in['Wq'], 'L1_cond_Wk': _L1_cond_in['Wk'], 'L1_cond_Wv': _L1_cond_in['Wv'], 'L1_cond_Wo': _L1_cond_in['Wo'], 'L1_cond_q_norm_w': _L1_cond_in['q_norm_w'], 'L1_cond_k_norm_w': _L1_cond_in['k_norm_w'], 'L1_cond_k_cache': _L1_cond_in['k_cache'], 'L1_cond_v_cache': _L1_cond_in['v_cache'], 'L1_ffn_W_base': _L1_ffn_in['W_base'], 'L1_ffn_b_base': _L1_ffn_in['b_base'], 'L1_ffn_W_router': _L1_ffn_in['W_router'], 'L1_ffn_A_stack': _L1_ffn_in['A_stack'], 'L1_ffn_B_stack': _L1_ffn_in['B_stack']}

def reference(x, itok_B_8_3872, itok_Bx16_0_63, itok_B_207_1644, L0_cond_log_dt, L0_cond_C, L0_cond_log_A_real, L0_cond_A_imag, L0_cond_D, L0_ffn_W_base, L0_ffn_b_base, L0_ffn_W_gate, L0_ffn_A, L0_ffn_B, L1_cond_Wq, L1_cond_Wk, L1_cond_Wv, L1_cond_Wo, L1_cond_q_norm_w, L1_cond_k_norm_w, L1_cond_k_cache, L1_cond_v_cache, L1_ffn_W_base, L1_ffn_b_base, L1_ffn_W_router, L1_ffn_A_stack, L1_ffn_B_stack):
    import jax
    import jax.numpy as jnp

    def _L0_cond_ref(u, length, log_dt, C, log_A_real, A_imag, D):
        import math
        import jax, jax.numpy as jnp
        import numpy as np
        H, N, B, L = (32, 64, 16, 512)
        DT_MIN, DT_MAX = (0.001, 0.1)

        def _get_kernel(log_dt, C, log_A_real, A_imag, length):
            Cc = C[..., 0] + 1j * C[..., 1]
            dt = jnp.exp(log_dt)
            A = -jnp.exp(log_A_real) + 1j * A_imag
            dtA = A * dt[:, None]
            P = dtA[:, :, None] * jnp.arange(length, dtype=jnp.float32)
            Cs = Cc * (jnp.exp(dtA) - 1.0) / A
            K = 2.0 * jnp.einsum('hn,hnl->hl', Cs, jnp.exp(P)).real
            return K
        Bq, Hq, Lq = u.shape
        mask = (jnp.arange(Lq) < length[:, None]).astype(u.dtype)
        u_m = u * mask[:, None, :]
        kernel = _get_kernel(log_dt, C, log_A_real, A_imag, Lq)
        n = 2 * Lq
        k_f = jnp.fft.rfft(kernel, n=n)
        u_f = jnp.fft.rfft(u_m, n=n)
        y = jnp.fft.irfft(u_f * k_f, n=n)[..., :Lq]
        y = y + u_m * D[:, None]
        return y * mask[:, None, :]

    def _L0_ffn_ref(x, W_base, b_base, W_gate, A, B):
        import jax, jax.numpy as jnp
        import numpy as np
        BATCH, TOK, DIM, OUT = (4, 256, 512, 512)
        E, R, TOP_K = (8, 16, 2)
        SCALING = 16.0 / R
        result = jnp.einsum('bnd,od->bno', x, W_base) + b_base
        logits = jnp.einsum('bnd,ed->bne', x, W_gate)
        probs = jax.nn.softmax(logits.astype(jnp.float32), axis=-1)
        top_p, top_i = jax.lax.top_k(probs, TOP_K)
        top_p = top_p / jnp.sum(top_p, axis=-1, keepdims=True)
        top_p = top_p.astype(x.dtype)
        route_w = jnp.sum(jax.nn.one_hot(top_i, E, dtype=x.dtype) * top_p[..., None], axis=-2)
        h = jnp.einsum('bnd,erd->bner', x, A)
        hw = h * route_w[..., None]
        delta = jnp.einsum('bner,eor->bno', hw, B)
        return result + delta * SCALING

    def _L1_cond_ref(x, Wq, Wk, Wv, Wo, q_norm_w, k_norm_w, k_cache, v_cache, block_table, cache_seqlens):
        import jax, jax.numpy as jnp
        import numpy as np
        B, S, HID = (4, 128, 512)
        D, HQ, HK = (128, 32, 8)
        PAGES, PSIZE, NPP = (64, 32, 16)
        THETA = 10000.0
        EPS = 1e-06
        SCALE = 1.0 / float(np.sqrt(D))

        def _rmsnorm(t, w):
            var = jnp.mean(t * t, axis=-1, keepdims=True)
            return t * jax.lax.rsqrt(var + EPS) * w

        def _rope(t, pos):
            inv_freq = 1.0 / THETA ** (jnp.arange(0, D, 2, dtype=jnp.float32) / D)
            freqs = pos[..., None].astype(jnp.float32) * inv_freq
            cos = jnp.cos(freqs)[:, :, None, :]
            sin = jnp.sin(freqs)[:, :, None, :]
            t1, t2 = (t[..., :D // 2], t[..., D // 2:])
            return jnp.concatenate([t1 * cos - t2 * sin, t2 * cos + t1 * sin], axis=-1)
        bsz, seqlen, _ = x.shape
        q = jnp.einsum('bsd,ed->bse', x, Wq).reshape(bsz, seqlen, HQ, D)
        k = jnp.einsum('bsd,ed->bse', x, Wk).reshape(bsz, seqlen, HK, D)
        v = jnp.einsum('bsd,ed->bse', x, Wv).reshape(bsz, seqlen, HK, D)
        q = _rmsnorm(q, q_norm_w)
        k = _rmsnorm(k, k_norm_w)
        pos = cache_seqlens[:, None] + jnp.arange(seqlen)[None, :]
        q = _rope(q, pos)
        k = _rope(k, pos)
        L = NPP * PSIZE
        kc = k_cache[block_table].reshape(bsz, L, HK, D)
        vc = v_cache[block_table].reshape(bsz, L, HK, D)
        k_all = jnp.concatenate([kc, k], axis=1)
        v_all = jnp.concatenate([vc, v], axis=1)
        valid_c = jnp.arange(L)[None, :] < cache_seqlens[:, None]
        valid = jnp.concatenate([valid_c, jnp.ones((bsz, seqlen), dtype=bool)], axis=1)
        rep = HQ // HK
        k_all = jnp.repeat(k_all, rep, axis=2)
        v_all = jnp.repeat(v_all, rep, axis=2)
        scores = jnp.einsum('bqhd,bkhd->bhqk', q, k_all) * SCALE
        scores = jnp.where(valid[:, None, None, :], scores, -1e+30)
        probs = jax.nn.softmax(scores, axis=-1)
        o = jnp.einsum('bhqk,bkhd->bqhd', probs, v_all)
        o = o.reshape(bsz, seqlen, HQ * D)
        return jnp.einsum('bse,de->bsd', o, Wo)

    def _L1_ffn_ref(x, W_base, b_base, W_router, A_stack, B_stack):
        import jax, jax.numpy as jnp
        import numpy as np
        D_IN = 512
        D_OUT = 512
        RANK = 16
        NUM_EXPERTS = 8
        TOP_K = 2
        SCALING = 32.0 / RANK
        orig_shape = x.shape
        xf = x.reshape(-1, D_IN)
        logits = xf @ W_router.T
        probs = jax.nn.softmax(logits, axis=-1)
        topk_p, topk_i = jax.lax.top_k(probs, TOP_K)
        topk_p = topk_p / jnp.sum(topk_p, axis=-1, keepdims=True)
        combine = jnp.sum(jax.nn.one_hot(topk_i, NUM_EXPERTS, dtype=xf.dtype) * topk_p[..., None], axis=1)
        h = jnp.einsum('nd,erd->ner', xf, A_stack)
        h = h * combine[..., None]
        lora_out = jnp.einsum('ner,eor->no', h, B_stack) * SCALING
        base_out = xf @ W_base.T + b_base
        out = base_out + lora_out
        return out.reshape(orig_shape[:-1] + (D_OUT,))
    x = x + _L0_ffn_ref(_L0_cond_ref(x, itok_B_8_3872, L0_cond_log_dt, L0_cond_C, L0_cond_log_A_real, L0_cond_A_imag, L0_cond_D), L0_ffn_W_base, L0_ffn_b_base, L0_ffn_W_gate, L0_ffn_A, L0_ffn_B)
    x = x + _L1_ffn_ref(_L1_cond_ref(x, L1_cond_Wq, L1_cond_Wk, L1_cond_Wv, L1_cond_Wo, L1_cond_q_norm_w, L1_cond_k_norm_w, L1_cond_k_cache, L1_cond_v_cache, itok_Bx16_0_63, itok_B_207_1644), L1_ffn_W_base, L1_ffn_b_base, L1_ffn_W_router, L1_ffn_A_stack, L1_ffn_B_stack)
    return x

_drawn_inputs = setup_inputs


def setup_inputs(seed=0):
    import zlib

    import numpy as np

    out = dict(_drawn_inputs(seed))
    spreads = {'L0_cond_log_A_real': (-0.6931471824645996, 0.2)}
    factors = {'L0_ffn_b_base': 8.0,
     'L1_cond_Wq': 2.712,
     'L1_cond_Wk': 8.0,
     'L1_cond_Wv': 8.0,
     'L1_cond_q_norm_w': 4.692,
     'L1_cond_k_norm_w': 8.0,
     'L1_cond_k_cache': 2.721,
     'L1_ffn_b_base': 200.0,
     'L1_ffn_W_router': 8.0,
     'L1_ffn_A_stack': 8.0,
     'L1_ffn_B_stack': 8.0}
    for name, (base, spread) in spreads.items():
        noise = np.random.default_rng([zlib.crc32(name.encode()), seed]).standard_normal(out[name].shape)
        drawn = base * np.exp(spread * noise) if base else spread * noise
        out[name] = jnp.asarray(drawn.astype(out[name].dtype))
    for name, factor in factors.items():
        out[name] = (out[name] * factor).astype(out[name].dtype)
    return out
```

```python
from contextlib import ExitStack
import math

import numpy as np

import concourse.bass as bass
from concourse import mybir

F32 = mybir.dt.float32
F32R = mybir.dt.float32r
I32 = mybir.dt.int32
U32 = mybir.dt.uint32
ALU = mybir.AluOpType
ACT = mybir.ActivationFunctionType
AX = mybir.AxisListType

P = 128
B, S, L = 64, 32, 512
T = B * S
KB = L // P
NS = 64
HP = S // 2
E, R = 8, 16
HQ, HK, D = 32, 8, 128
REP = HQ // HK
PAGES, PSIZE, NPP = 64, 32, 16
LK = NPP * PSIZE
NKEY = LK + S
NT = T // P
BPT = P // S
KC = LK // P
NQU = HK + HK // REP
THETA, EPS = 10000.0, 1e-6
NEG = -1e30
KPW = P + L

MAGIC = 1.5 * 2.0 ** 23
LN2_HI, LN2_LO = 0.693359375, -2.12194440e-4
TWO_PI_1 = 6.28125
TWO_PI_2 = float(np.float32(math.floor((2 * math.pi - TWO_PI_1) * 2 ** 20) / 2 ** 20))
TWO_PI_3 = 2 * math.pi - TWO_PI_1 - TWO_PI_2
PI_SAFE = 3.1415925

NMUL = 48
C_ID = 0
C_IOTA = C_ID + P
C_EXPAND = C_IOTA + LK
C_FREQ = C_EXPAND + P
C_MUL = C_FREQ + D // 2
C_DESC = C_MUL + NMUL
C_ROW = C_DESC + E
C_REV = C_ROW + KB
C_MOD = C_REV + KB
C_ALL = C_MOD + 1


def constants():
    c = np.zeros((P, C_ALL), np.float32)
    c[:, C_ID:C_ID + P] = np.eye(P)
    c[:, C_IOTA:C_IOTA + LK] = np.arange(LK)
    for e in range(E):
        c[e, C_EXPAND + e * R:C_EXPAND + (e + 1) * R] = 1.0
    exponents = np.arange(0, D, 2, dtype=np.float32) / np.float32(D)
    c[:, C_FREQ:C_FREQ + D // 2] = np.float32(1.0) / np.power(np.float32(THETA), exponents)
    c[:, C_MUL:C_MUL + 32] = np.arange(32)
    c[:, C_MUL + 32:C_MUL + 48] = 32 * np.arange(16)
    c[:, C_DESC:C_DESC + E] = E - np.arange(E)
    for k in range(KB):
        c[:, C_ROW + k] = k * P + np.arange(P)
        c[:, C_REV + k] = k * P + P - 1 - np.arange(P)
    c[:, C_MOD] = np.arange(P) % S
    return c


class Line:

    def __init__(self, eng, sem):
        self.eng, self.sem, self.n = eng, sem, 0

    def __call__(self, ins):
        ins.then_inc(self.sem, 1)
        self.n += 1
        self.eng.wait_ge(self.sem, self.n)


def credits(eng, sem, n):
    for _ in range(n):
        eng.nop().then_inc(sem, 1)


def spread(ap, axis, n):
    ap = ap.unsqueeze(axis)
    shape = list(ap.shape)
    shape[axis] = n
    return ap.to_broadcast(shape)


def exp_exact(v, x, out, t, k, p):
    v(lambda e: e.tensor_scalar(x, x, 88.0, -87.0, ALU.min, ALU.max))
    v(lambda e: e.tensor_scalar(t, x, 1.0 / math.log(2.0), MAGIC + 127.0, ALU.mult, ALU.add))
    v(lambda e: e.tensor_scalar(k, t, MAGIC + 127.0, None, ALU.subtract))
    v(lambda e: e.scalar_tensor_tensor(out=x, in0=k, scalar=-LN2_HI, in1=x, op0=ALU.mult, op1=ALU.add))
    v(lambda e: e.scalar_tensor_tensor(out=x, in0=k, scalar=-LN2_LO, in1=x, op0=ALU.mult, op1=ALU.add))
    v(lambda e: e.tensor_scalar(p, x, 1.0 / 5040.0, None, ALU.mult))
    for c in (1 / 720, 1 / 120, 1 / 24, 1 / 6, 0.5, 1.0):
        v(lambda e, c=c: e.scalar_tensor_tensor(out=p, in0=p, scalar=c, in1=x, op0=ALU.add, op1=ALU.mult))
    v(lambda e: e.tensor_scalar(k.bitcast(I32), t.bitcast(I32), 23, None, ALU.logical_shift_left))
    v(lambda e: e.scalar_tensor_tensor(out=out, in0=p, scalar=1.0, in1=k, op0=ALU.add, op1=ALU.mult))


def reduce_angle(v, f, t, sin_arg, cos_arg):
    v(lambda e: e.tensor_scalar(t, f, 1.0 / (2 * math.pi), MAGIC, ALU.mult, ALU.add))
    v(lambda e: e.tensor_scalar(t, t, MAGIC, None, ALU.subtract))
    v(lambda e: e.scalar_tensor_tensor(out=f, in0=t, scalar=-TWO_PI_1, in1=f, op0=ALU.mult, op1=ALU.add))
    v(lambda e: e.scalar_tensor_tensor(out=f, in0=t, scalar=-TWO_PI_2, in1=f, op0=ALU.mult, op1=ALU.add))
    v(lambda e: e.scalar_tensor_tensor(out=f, in0=t, scalar=-TWO_PI_3, in1=f, op0=ALU.mult, op1=ALU.add))
    v(lambda e: e.tensor_scalar(sin_arg, f, PI_SAFE, -PI_SAFE, ALU.min, ALU.max))
    v(lambda e: e.scalar_tensor_tensor(out=cos_arg, in0=sin_arg, scalar=-1.0, in1=sin_arg, op0=ALU.mult, op1=ALU.max))
    v(lambda e: e.tensor_scalar(cos_arg, cos_arg, -1.0, math.pi / 2, ALU.mult, ALU.add))


def s4d_taps(nc, ps, dram, taps):
    with ExitStack() as ctx:
        sb = lambda n, s, d=F32: ctx.enter_context(nc.sbuf_tensor("s4_" + n, s, d))
        sem = lambda n: ctx.enter_context(nc.semaphore("s4_" + n))
        cst = sb("cst", [P, C_ALL])
        raw = sb("raw", [P, 2, HP])
        ex = sb("ex", [P, 2, HP])
        ai = sb("ai", [P, HP])
        cc = sb("cc", [P, HP, 2])
        dvec = sb("dvec", [1, S])
        small = sb("small", [P, 12, HP])
        shape = [P, HP, NMUL]
        arg, mag, t1, t2, t3, ang, sa, ca, sn, cs, er, ei = (
            sb(n, shape) for n in ("arg", "mag", "t1", "t2", "t3", "ang", "sa", "ca", "sn", "cs", "er", "ei"))
        ur, ui, ut = (sb(n, [P, HP, 16]) for n in ("ur", "ui", "ut"))
        kev = sb("kev", [16, HP, 2, 32])
        zeros = sb("zeros", [S, P])
        s_in, s_v, s_sin, s_u, s_k, s_ev, s_out = (
            sem(n) for n in ("in", "v", "sin", "u", "k", "ev", "out"))
        done = {}
        mul = cst[:, C_MUL:C_MUL + NMUL]
        with nc.Block() as block:
            @block.sync
            def _(e):
                e.dma_start(cst[:, :], dram["cst"]).then_inc(s_in, 16)
                for half in range(2):
                    src = bass.AP(tensor=dram["L0_cond_log_dt"].tensor, offset=half, ap=[[0, NS], [2, HP]])
                    e.dma_start(raw[half * NS:(half + 1) * NS, 0, :], src, allow_slow_non_contiguous=True).then_inc(s_in, 16)
                e.dma_start(raw[:, 1, :], dram["log_a"]).then_inc(s_in, 16)
                e.dma_start(ai[:, :], dram["a_imag"]).then_inc(s_in, 16)
                e.dma_start(cc[:, :, :], dram["c"]).then_inc(s_in, 16)
                e.dma_start(dvec[:, :], dram["L0_cond_D"].rearrange("(o h) -> o h", o=1)).then_inc(s_in, 16)
                e.wait_ge(s_ev, 1)
                e.dma_start(taps[:, P:KPW].rearrange("h (a b) -> a h b", b=32),
                            kev[:, :, :, :].rearrange("a i t b -> a (i t) b")).then_inc(s_out, 16)
                e.dma_start(taps[:, 0:P], zeros[:, :]).then_inc(s_out, 16)
                e.wait_ge(s_out, 32)

            @block.vector
            def _(e):
                line = Line(e, s_v)
                v = lambda f: line(f(e))
                v(lambda e: e.memset(zeros[:, :], 0.0))
                e.wait_ge(s_in, 16 * 7)
                flat = lambda x: x.rearrange("p a b -> p (a b)")
                w = [small[:, i, :] for i in range(12)]
                tmp = small[:, 6:12, :]
                exp_exact(v, flat(raw[:, :, :]), flat(ex[:, :, :]), flat(tmp[:, 0:2, :]),
                          flat(tmp[:, 2:4, :]), flat(tmp[:, 4:6, :]))
                ar, dar, dai = w[0], w[1], w[2]
                v(lambda e: e.tensor_scalar(ar, ex[:, 1, :], -1.0, None, ALU.mult))
                v(lambda e: e.tensor_tensor(dar, ar, ex[:, 0, :], ALU.mult))
                v(lambda e: e.tensor_tensor(dai, ai[:, :], ex[:, 0, :], ALU.mult))
                mulb = spread(mul, 1, HP)
                v(lambda e: e.tensor_tensor(ang[:, :, :], spread(dai, 2, NMUL), mulb, ALU.mult))
                reduce_angle(v, flat(ang[:, :, :]), flat(t1[:, :, :]), flat(sa[:, :, :]), flat(ca[:, :, :]))
                done["angles"] = line.n
                v(lambda e: e.tensor_tensor(arg[:, :, :], spread(dar, 2, NMUL), mulb, ALU.mult))
                exp_exact(v, flat(arg[:, :, :]), flat(mag[:, :, :]), flat(t1[:, :, :]), flat(t2[:, :, :]), flat(t3[:, :, :]))
                e.wait_ge(s_sin, 2)
                v(lambda e: e.tensor_tensor(er[:, :, :], mag[:, :, :], cs[:, :, :], ALU.mult))
                v(lambda e: e.tensor_tensor(ei[:, :, :], mag[:, :, :], sn[:, :, :], ALU.mult))
                zr, zi, nr, ni, t, u = w[3], ei[:, :, 1], w[4], w[5], w[6], w[7]
                cr, ci = cc[:, :, 0], cc[:, :, 1]
                v(lambda e: e.tensor_scalar(zr, er[:, :, 1], 1.0, None, ALU.subtract))
                v(lambda e: e.tensor_tensor(nr, cr, zr, ALU.mult))
                v(lambda e: e.tensor_tensor(t, ci, zi, ALU.mult))
                v(lambda e: e.tensor_tensor(nr, nr, t, ALU.subtract))
                v(lambda e: e.tensor_tensor(ni, cr, zi, ALU.mult))
                v(lambda e: e.tensor_tensor(t, ci, zr, ALU.mult))
                v(lambda e: e.tensor_tensor(ni, ni, t, ALU.add))
                sr, si, den = w[8], w[9], w[10]
                v(lambda e: e.tensor_tensor(sr, nr, ar, ALU.mult))
                v(lambda e: e.tensor_tensor(t, ni, ai[:, :], ALU.mult))
                v(lambda e: e.tensor_tensor(sr, sr, t, ALU.add))
                v(lambda e: e.tensor_tensor(si, ni, ar, ALU.mult))
                v(lambda e: e.tensor_tensor(t, nr, ai[:, :], ALU.mult))
                v(lambda e: e.tensor_tensor(si, si, t, ALU.subtract))
                v(lambda e: e.tensor_tensor(den, ar, ar, ALU.mult))
                v(lambda e: e.tensor_tensor(t, ai[:, :], ai[:, :], ALU.mult))
                v(lambda e: e.tensor_tensor(den, den, t, ALU.add))
                v(lambda e: e.reciprocal(u, den))
                v(lambda e: e.scalar_tensor_tensor(out=sr, in0=sr, scalar=2.0, in1=u, op0=ALU.mult, op1=ALU.mult))
                v(lambda e: e.scalar_tensor_tensor(out=si, in0=si, scalar=2.0, in1=u, op0=ALU.mult, op1=ALU.mult))
                ear, eai = er[:, :, 32:48], ei[:, :, 32:48]
                srb, sib = spread(sr, 2, 16), spread(si, 2, 16)
                v(lambda e: e.tensor_tensor(ur[:, :, :], srb, ear, ALU.mult))
                v(lambda e: e.tensor_tensor(ut[:, :, :], sib, eai, ALU.mult))
                v(lambda e: e.tensor_tensor(ur[:, :, :], ur[:, :, :], ut[:, :, :], ALU.subtract))
                v(lambda e: e.tensor_tensor(ui[:, :, :], srb, eai, ALU.mult))
                v(lambda e: e.tensor_tensor(ut[:, :, :], sib, ear, ALU.mult))
                e.scalar_tensor_tensor(out=ui[:, :, :], in0=ui[:, :, :], scalar=-1.0, in1=ut[:, :, :],
                                       op0=ALU.mult, op1=ALU.subtract).then_inc(s_u, 1)
                e.wait_ge(s_k, 1)
                for half in range(2):
                    v(lambda e: e.tensor_copy(kev[:, :, half, :], ps[0:16, half, :].rearrange("a (i b) -> a i b", b=32)))
                d = kev[0:1, :, :, 0:1].rearrange("a i t b -> a (i t b)")
                e.tensor_tensor(d, d, dvec[:, :], ALU.add).then_inc(s_ev, 1)

            @block.scalar
            def _(e):
                e.wait_ge(s_v, done["angles"])
                e.activation(sn[:, :, :], sa[:, :, :], ACT.Sin).then_inc(s_sin, 1)
                e.activation(cs[:, :, :], ca[:, :, :], ACT.Sin).then_inc(s_sin, 1)

            @block.tensor
            def _(e):
                e.wait_ge(s_u, 1)
                for half in range(2):
                    rows = slice(half * NS, (half + 1) * NS)
                    for i in range(HP):
                        out = ps[0:16, half, i * 32:(i + 1) * 32]
                        e.matmul(out, ur[rows, i, :], er[rows, i, 0:32], start=True, stop=False)
                        last = e.matmul(out, ui[rows, i, :], ei[rows, i, 0:32], start=False, stop=True)
                last.then_inc(s_k, 1)


def convolve(nc, ps, dram, taps, y_t):
    with ExitStack() as ctx:
        sb = lambda n, s, d=F32: ctx.enter_context(nc.sbuf_tensor("cv_" + n, s, d))
        sem = lambda n: ctx.enter_context(nc.semaphore("cv_" + n))
        cst = sb("cst", [P, C_ALL])
        um = sb("um", [P, KB, S, B])
        leni = sb("leni", [P, B], I32)
        lenf = sb("lenf", [P, B])
        mrev = sb("mrev", [P, KB, B])
        mrow = sb("mrow", [P, KB, B])
        toe = sb("toe", [P, 2, L])
        s_in, s_x, s_v, s_um, s_mm, s_y = (sem(n) for n in ("in", "x", "v", "um", "mm", "y"))
        s_toe = [sem("toe0"), sem("toe1")]
        y_v = y_t[:, :, :].rearrange("p k (b h) -> p k b h", h=S)

        def load(e, h, q):
            src = bass.AP(tensor=taps.tensor, offset=h * KPW + 1, ap=[[1, P], [1, L]])
            e.dma_start(toe[:, q, :], src).then_inc(s_toe[q], 16)

        with nc.Block() as block:
            @block.sync
            def _(e):
                e.dma_start(cst[:, :], dram["cst"]).then_inc(s_in, 16)
                src = bass.AP(tensor=dram["itok_B_8_3872"].tensor, offset=0, ap=[[0, P], [1, B]])
                e.dma_start(leni[:, :], src).then_inc(s_in, 16)
                for k in range(KB):
                    e.dma_start(um[:, k, :, :], dram["x_rev"][k * P:(k + 1) * P, :, :]).then_inc(s_x, 16)
                load(e, 0, 0)
                load(e, 1, 1)
                with e.Fori(0, S // 2 - 1) as i:
                    for q in range(2):
                        e.wait_ge(s_mm, i * 2 + q + 1)
                        load(e, i * 2 + q + 2, q)

            @block.vector
            def _(e):
                line = Line(e, s_v)
                v = lambda f: line(f(e))
                e.wait_ge(s_in, 32)
                v(lambda e: e.tensor_copy(lenf[:, :], leni[:, :]))
                for k in range(KB):
                    v(lambda e: e.tensor_scalar(mrev[:, k, :], lenf[:, :], cst[:, C_REV + k:C_REV + k + 1], None, ALU.is_gt))
                    v(lambda e: e.tensor_scalar(mrow[:, k, :], lenf[:, :], cst[:, C_ROW + k:C_ROW + k + 1], None, ALU.is_gt))
                e.wait_ge(s_x, 16 * KB)
                for k in range(KB):
                    e.tensor_tensor(um[:, k, :, :], um[:, k, :, :], spread(mrev[:, k, :], 1, S), ALU.mult).then_inc(s_um, 1)
                credits(e, s_y, 2)
                with e.Fori(0, S // 2) as i:
                    for q in range(2):
                        e.wait_ge(s_mm, i * 2 + q + 1)
                        e.tensor_tensor(y_v[:, :, :, bass.ds(i * 2 + q, 1)].rearrange("p k b o -> p k (b o)"),
                                        ps[:, q, 0:KB * B].rearrange("p (k b) -> p k b", k=KB),
                                        mrow[:, :, :], ALU.mult).then_inc(s_y, 1)

            @block.tensor
            def _(e):
                e.wait_ge(s_um, KB)
                with e.Fori(0, S // 2) as i:
                    for q in range(2):
                        e.wait_ge(s_toe[q], i * 16 + 16)
                        e.wait_ge(s_y, i * 2 + q + 1)
                        for lb in range(KB):
                            for mb in range(lb + 1):
                                last = e.matmul(ps[:, q, lb * B:(lb + 1) * B],
                                                toe[:, q, (lb - mb) * P:(lb - mb + 1) * P],
                                                um[:, mb, bass.ds(i * 2 + q, 1), :].rearrange("p o b -> p (o b)"),
                                                start=(mb == 0), stop=(mb == lb))
                        last.then_inc(s_mm, 1)


def ffn(nc, ps, dram, names, tag, act, resid, scaling, out=None):
    w_n, b_n, g_n, a_n, lb_n = names
    NB = T // 512
    with ExitStack() as ctx:
        sb = lambda n, s, d=F32: ctx.enter_context(nc.sbuf_tensor(f"f{tag}_{n}", s, d))
        sem = lambda n: ctx.enter_context(nc.semaphore(f"f{tag}_{n}"))
        cst = sb("cst", [P, C_ALL])
        w = sb("w", [P, KB, L])
        a = sb("a", [P, KB, E * R])
        g = sb("g", [P, KB, E])
        lb = sb("lb", [E * R, L])
        bias = sb("bias", [P, KB])
        lg, eq, one1, one2, l2 = (sb(n, [P, NT, E]) for n in ("lg", "eq", "one1", "one2", "l2"))
        m1, m2, fm, d, e2, p1, p2 = (sb(n, [P, NT]) for n in ("m1", "m2", "fm", "d", "e2", "p1", "p2"))
        route = sb("route", [P, NT, E])
        route_t = sb("route_t", [E, T])
        wexp = sb("wexp", [E * R, 512])
        hw = sb("hw", [E * R, 512])
        s_in, s_lg, s_v, s_d, s_e2, s_rt, s_rte, s_we, s_wx, s_h, s_hw, s_mm, s_ev, s_out = (sem(n) for n in (
            "in", "lg", "v", "d", "e2", "rt", "rte", "we", "wx", "h", "hw", "mm", "ev", "out"))
        done = {}
        with nc.Block() as block:
            @block.sync
            def _(e):
                e.dma_start(cst[:, :], dram["cst"]).then_inc(s_in, 16)
                e.dma_start(g[:, :, :], dram[g_n].rearrange("(k p) e -> p k e", p=P)).then_inc(s_in, 16)
                e.dma_start(bias[:, :], dram[b_n]).then_inc(s_in, 16)
                e.dma_start(w[:, :, :], dram[w_n].rearrange("(k p) o -> p k o", p=P)).then_inc(s_in, 16)
                e.dma_start(a[:, :, :], dram[a_n].rearrange("(k p) r -> p k r", p=P)).then_inc(s_in, 16)
                e.dma_start(lb[:, :], dram[lb_n]).then_inc(s_in, 16)
                if out is not None:
                    for i in range(NB):
                        for ob in range(KB):
                            e.wait_ge(s_ev, KB + KB * i + ob + 1)
                            e.dma_start(out[ob * P:(ob + 1) * P, i * 512:(i + 1) * 512],
                                        resid[:, ob, i * 512:(i + 1) * 512]).then_inc(s_out, 16)
                    e.wait_ge(s_out, 16 * NB * KB)

            @block.vector
            def _(e):
                line = Line(e, s_v)
                v = lambda f: line(f(e))
                e.wait_ge(s_in, 16 * 6)
                e.wait_ge(s_lg, 1)
                v(lambda e: e.tensor_copy(lg[:, :, :], ps[:, 0, 0:NT * E].rearrange("p (t e) -> p t e", e=E)))
                desc = spread(cst[:, C_DESC:C_DESC + E], 1, NT)

                def pick(logits, m, one):
                    v(lambda e: e.tensor_reduce(m[:, :], logits[:, :, :], AX.X, ALU.max))
                    v(lambda e: e.tensor_tensor(eq[:, :, :], logits[:, :, :], spread(m[:, :], 2, E), ALU.is_equal))
                    v(lambda e: e.tensor_tensor(eq[:, :, :], eq[:, :, :], desc, ALU.mult))
                    v(lambda e: e.tensor_reduce(fm[:, :], eq[:, :, :], AX.X, ALU.max))
                    v(lambda e: e.tensor_tensor(one[:, :, :], desc, spread(fm[:, :], 2, E), ALU.is_equal))

                pick(lg, m1, one1)
                v(lambda e: e.scalar_tensor_tensor(out=l2[:, :, :], in0=one1[:, :, :], scalar=-3e38, in1=lg[:, :, :],
                                                   op0=ALU.mult, op1=ALU.add))
                pick(l2, m2, one2)
                v(lambda e: e.tensor_tensor(d[:, :], m2[:, :], m1[:, :], ALU.subtract))
                done["gap"] = line.n
                e.wait_ge(s_e2, 1)
                v(lambda e: e.tensor_scalar(p1[:, :], e2[:, :], 1.0, None, ALU.add))
                v(lambda e: e.reciprocal(p1[:, :], p1[:, :]))
                v(lambda e: e.tensor_tensor(p2[:, :], e2[:, :], p1[:, :], ALU.mult))
                v(lambda e: e.tensor_tensor(one1[:, :, :], one1[:, :, :], spread(p1[:, :], 2, E), ALU.mult))
                v(lambda e: e.tensor_tensor(one2[:, :, :], one2[:, :, :], spread(p2[:, :], 2, E), ALU.mult))
                v(lambda e: e.tensor_tensor(route[:, :, :], one1[:, :, :], one2[:, :, :], ALU.add))
                done["route"] = line.n
                e.wait_ge(s_rt, 1)
                for c in range(NB):
                    last = e.tensor_copy(route_t[:, c * 512:(c + 1) * 512], ps[0:E, 1 + c, :])
                last.then_inc(s_rte, 1)
                credits(e, s_ev, KB)
                with e.Fori(0, NB) as i:
                    e.wait_ge(s_wx, i + 1)
                    e.wait_ge(s_h, i + 1)
                    e.scalar_tensor_tensor(out=hw[:, :], in0=ps[:, 6, :], scalar=scaling, in1=wexp[:, :],
                                           op0=ALU.mult, op1=ALU.mult).then_inc(s_hw, 1)
                    for ob in range(KB):
                        r = resid[:, ob, bass.ds(i * 512, 512)]
                        e.wait_ge(s_mm, i * KB + ob + 1)
                        e.scalar_tensor_tensor(out=r, in0=ps[:, 1 + ob, :], scalar=bias[:, ob:ob + 1], in1=r,
                                               op0=ALU.add, op1=ALU.add).then_inc(s_ev, 1)

            @block.scalar
            def _(e):
                e.wait_ge(s_v, done["gap"])
                e.activation(e2[:, :], d[:, :], ACT.Exp).then_inc(s_e2, 1)
                with e.Fori(0, NB) as i:
                    e.wait_ge(s_hw, i)
                    e.wait_ge(s_we, i + 1)
                    e.activation(wexp[:, :], ps[:, 5, :], ACT.Copy).then_inc(s_wx, 1)

            @block.tensor
            def _(e):
                e.wait_ge(s_in, 16 * 6)
                for t in range(NT):
                    for k in range(KB):
                        last = e.matmul(ps[:, 0, t * E:(t + 1) * E], act[:, k, t * P:(t + 1) * P], g[:, k, :],
                                        start=(k == 0), stop=(k == KB - 1))
                last.then_inc(s_lg, 1)
                e.wait_ge(s_v, done["route"])
                for t in range(NT):
                    last = e.transpose(ps[0:E, 1 + t // 4, (t % 4) * P:(t % 4 + 1) * P], route[:, t, :],
                                       cst[:, C_ID:C_ID + P])
                last.then_inc(s_rt, 1)
                e.wait_ge(s_rte, 1)
                with e.Fori(0, NB) as i:
                    cols = bass.ds(i * 512, 512)
                    e.wait_ge(s_wx, i)
                    e.matmul(ps[:, 5, :], cst[0:E, C_EXPAND:C_EXPAND + P], route_t[:, cols],
                             start=True, stop=True).then_inc(s_we, 1)
                    e.wait_ge(s_hw, i)
                    for k in range(KB):
                        last = e.matmul(ps[:, 6, :], a[:, k, :], act[:, k, cols], start=(k == 0), stop=(k == KB - 1))
                    last.then_inc(s_h, 1)
                    for ob in range(KB):
                        e.wait_ge(s_ev, i * KB + ob + 1)
                        for k in range(KB):
                            e.matmul(ps[:, 1 + ob, :], w[:, k, ob * P:(ob + 1) * P], act[:, k, cols],
                                     start=(k == 0), stop=False)
                    e.wait_ge(s_hw, i + 1)
                    for ob in range(KB):
                        e.matmul(ps[:, 1 + ob, :], lb[:, ob * P:(ob + 1) * P], hw[:, :],
                                 start=False, stop=True).then_inc(s_mm, 1)


def wait(eng, sem, value):
    if not isinstance(value, int) or value > 0:
        eng.wait_ge(sem, value)


def pipeline(eng, units, per, lead, step):
    for u in range(lead):
        step(0, u, u, True, False)
    with eng.Fori(0, units // per - 1) as i:
        for j in range(lead, per + lead):
            step(i, j, i * per + j, True, True)
    i = units // per - 1
    for j in range(lead, per + lead):
        step(i, j, i * per + j, j < per, True)


def wait_apart(eng, sem_passed, *waits):
    for sem, v in waits:
        wait(eng, sem, v)
    eng.sem_inc(sem_passed, 1)


def turns(eng, units, per, lead, step):
    for u in range(lead):
        step(0, u, u, lambda off: u - off >= 0)
    with eng.Fori(0, units // per - 1) as i:
        for j in range(lead, per + lead):
            step(i, j, i * per + j, lambda off: True)
    i = units // per - 1
    for j in range(lead, per + lead):
        step(i, j, i * per + j, lambda off: j - off < per)


def rope_angles(nc, dram, cos, sin):
    with ExitStack() as ctx:
        sb = lambda n, s, d=F32: ctx.enter_context(nc.sbuf_tensor("ra_" + n, s, d))
        sem = lambda n: ctx.enter_context(nc.semaphore("ra_" + n))
        H = D // 2
        cst = sb("cst", [P, C_ALL])
        leni = sb("leni", [P, NT], I32)
        pos = sb("pos", [P, NT])
        f, t, sa, ca = (sb(n, [P, NT, H]) for n in ("f", "t", "sa", "ca"))
        s_in, s_v, s_sin = (sem(n) for n in ("in", "v", "sin"))
        done = {}
        flat = lambda x: x[:, :, :].rearrange("p a b -> p (a b)")
        with nc.Block() as block:
            @block.sync
            def _(e):
                e.dma_start(cst[:, :], dram["cst"]).then_inc(s_in, 16)
                for q in range(BPT):
                    src = bass.AP(tensor=dram["itok_B_207_1644"].tensor, offset=q, ap=[[0, S], [BPT, NT]])
                    e.dma_start(leni[q * S:(q + 1) * S, :], src, allow_slow_non_contiguous=True).then_inc(s_in, 16)

            @block.vector
            def _(e):
                line = Line(e, s_v)
                v = lambda g: line(g(e))
                e.wait_ge(s_in, 16 * (1 + BPT))
                v(lambda e: e.tensor_copy(pos[:, :], leni[:, :]))
                v(lambda e: e.tensor_scalar(pos[:, :], pos[:, :], cst[:, C_MOD:C_MOD + 1], None, ALU.add))
                v(lambda e: e.tensor_tensor(f[:, :, :], spread(pos[:, :], 2, H),
                                            spread(cst[:, C_FREQ:C_FREQ + H], 1, NT), ALU.mult))
                reduce_angle(v, flat(f), flat(t), flat(sa), flat(ca))
                done["angles"] = line.n

            @block.scalar
            def _(e):
                e.wait_ge(s_v, done["angles"])
                e.activation(sin[:, :, :], sa[:, :, :], ACT.Sin).then_inc(s_sin, 1)
                e.activation(cos[:, :, :], ca[:, :, :], ACT.Sin).then_inc(s_sin, 1)
                e.wait_ge(s_sin, 2)


class Weights:

    def __init__(self, nc, ctx, tag, src):
        self.src = src
        self.raw = ctx.enter_context(nc.sbuf_tensor(f"{tag}_raw", [P, KB, 512], F32))
        self.hi = ctx.enter_context(nc.sbuf_tensor(f"{tag}_hi", [P, 2 * KB, 512], F32R))
        self.lo = ctx.enter_context(nc.sbuf_tensor(f"{tag}_lo", [P, 2 * KB, 512], F32R))
        self.s_raw, self.s_hi, self.s_lo, self.s_passed = (
            ctx.enter_context(nc.semaphore(f"{tag}_{n}")) for n in ("s_raw", "s_hi", "s_lo", "s_passed"))

    def load(self, e, c, chunk):
        wait(e, self.s_lo, c * KB)
        src = self.src[bass.ds(chunk, 1), :, :] if not isinstance(chunk, int) else self.src[chunk:chunk + 1, :, :]
        e.dma_start(self.raw[:, :, :], src.rearrange("o (k p) n -> p (o k) n", p=P)).then_inc(self.s_raw, 16)

    def halve(self, e, c, k):
        row = (c % 2) * KB + k
        row = slice(row, row + 1) if isinstance(row, int) else bass.ds(row, 1)
        pick = lambda a: a[:, row, :].rearrange("p o n -> p (o n)")
        wait_apart(e, self.s_passed, (self.s_raw, c * 16 + 16))
        e.tensor_copy(pick(self.hi), self.raw[:, k, :]).then_inc(self.s_hi, 1)
        wait_apart(e, self.s_passed, (self.s_hi, c * KB + k + 1))
        e.tensor_tensor(pick(self.lo), self.raw[:, k, :], pick(self.hi).bitcast(F32), ALU.subtract).then_inc(self.s_lo, 1)

    def multiply(self, e, out, xh, xl, t, c):
        par = (c % 2) * KB
        for k in range(KB):
            w = slice(par + k, par + k + 1) if isinstance(par, int) else bass.ds(par + k, 1)
            hi = self.hi[:, w, :].rearrange("p o n -> p (o n)")
            lo = self.lo[:, w, :].rearrange("p o n -> p (o n)")
            cols = slice(t * P, (t + 1) * P)
            e.matmul(out, xh[:, k, cols], hi, start=(k == 0), stop=False)
            e.matmul(out, xh[:, k, cols], lo, start=False, stop=False)
            last = e.matmul(out, xl[:, k, cols], hi, start=False, stop=(k == KB - 1))
        return last


def project_rope(nc, ps, dram, tag, xh, xl, cos, sin, chunk0, chunks, norm, qk_t):
    H = D // 2
    with ExitStack() as ctx:
        sb = lambda n, s, d=F32: ctx.enter_context(nc.sbuf_tensor(f"{tag}_{n}", s, d))
        sem = lambda n: ctx.enter_context(nc.semaphore(f"{tag}_s_{n}"))
        w = Weights(nc, ctx, tag, dram["wqkv"])
        cst = sb("cst", [P, P])
        nw = sb("nw", [P, D])
        ta, tb = sb("ta", [P, NT, D]), sb("tb", [P, NT, D])
        sq, qn, m1, m2, qr, stage = (sb(n, [P, 2, 512]) for n in ("sq", "qn", "m1", "m2", "qr", "stage"))
        ss, rt, rs = (sb(n, [P, 2, REP]) for n in ("ss", "rt", "rs"))
        s_in, s_tab, s_proj, s_sq, s_red, s_ms, s_rt, s_rs, s_qn, s_m1, s_m2, s_qr, s_t, s_stage = (
            sem(n) for n in ("in", "tab", "proj", "sq", "red", "ms", "rt", "rs", "qn", "m1", "m2", "qr", "t", "stage"))
        s_st = [sem("st0"), sem("st1")]
        units, lead = chunks * NT, 2
        heads = lambda a: a.rearrange("p (h x) -> p h x", h=REP)
        with nc.Block() as block:
            @block.sync
            def _(e):
                w.load(e, 0, chunk0)
                e.dma_start(cst[:, :], dram["cst"][:, C_ID:C_ID + P]).then_inc(s_in, 16)
                e.dma_start(nw[:, :], bass.AP(tensor=dram[norm].tensor, offset=0, ap=[[0, P], [1, D]])).then_inc(s_in, 16)

                def stores(c):
                    for t in range(NT):
                        q = t % 2
                        e.wait_ge(s_stage, c * NT + t + 1 + 2)
                        cols = bass.ds(c * P + chunk0 * P, P) if not isinstance(c, int) else slice((c + chunk0) * P, (c + chunk0 + 1) * P)
                        e.dma_start(qk_t[t * BPT:(t + 1) * BPT, :, cols].rearrange("b d x -> d b x"),
                                    stage[:, q, :].rearrange("p (b x) -> p b x", b=BPT)).then_inc(s_st[q], 16)

                with e.Fori(0, chunks - 1) as c:
                    w.load(e, c + 1, c + (chunk0 + 1))
                    stores(c)
                stores(chunks - 1)
                for q in range(2):
                    e.wait_ge(s_st[q], 16 * units // 2)

            @block.gpsimd
            def _(e):
                e.wait_ge(s_in, 32)
                w1, w2 = spread(nw[:, 0:H], 1, NT), spread(nw[:, H:D], 1, NT)
                e.tensor_tensor(ta[:, :, 0:H], cos[:, :, :], w1, ALU.mult).then_inc(s_tab, 1)
                e.tensor_tensor(ta[:, :, H:D], cos[:, :, :], w2, ALU.mult).then_inc(s_tab, 1)
                e.tensor_tensor(tb[:, :, H:D], sin[:, :, :], w1, ALU.mult).then_inc(s_tab, 1)
                e.tensor_tensor(tb[:, :, 0:H], sin[:, :, :], w2, ALU.mult).then_inc(s_tab, 1)
                e.wait_ge(s_tab, 4)
                e.tensor_scalar(tb[:, :, 0:H], tb[:, :, 0:H], -1.0, None, ALU.mult).then_inc(s_tab, 1)
                e.wait_ge(s_tab, 5)
                for k in range(KB):
                    w.halve(e, 0, k)

                def step(i, j, u, new, old):
                    t, q = j % NT, j % 2
                    if not new:
                        return
                    for half in range(2):
                        a, b = slice(half * H, half * H + H), slice(H - half * H, D - half * H)
                        if half == 0:
                            wait_apart(e, w.s_passed, (s_qr, u - 1), (s_qn, u + 1))
                        ins = e.tensor_tensor(heads(m2[:, q, :])[:, :, a], heads(qn[:, q, :])[:, :, b],
                                              spread(tb[:, t, a], 1, REP), ALU.mult)
                    ins.then_inc(s_m2, 1)
                    if t % KB == 2 and not (isinstance(i, int) and i + 1 >= chunks):
                        w.halve(e, i + 1, t // KB)

                pipeline(e, units, NT, lead, step)

            @block.tensor
            def _(e):
                e.wait_ge(s_in, 32)

                def step(i, j, u, new, old):
                    t, q = j % NT, j % 2
                    if new:
                        if t == 0:
                            e.wait_ge(w.s_lo, (i + (j // NT) + 1) * KB)
                        wait(e, s_qn, u - 1)
                        w.multiply(e, ps[:, q, :], xh, xl, t, i + j // NT).then_inc(s_proj, 1)
                    if old:
                        e.wait_ge(s_stage, u - lead + 1)
                        e.wait_ge(s_qr, u - lead + 1)
                        for h in range(REP):
                            last = e.transpose(ps[:, 2 + q, h * P:(h + 1) * P], qr[:, q, h * D:(h + 1) * D], cst[:, :])
                        last.then_inc(s_t, 1)

                pipeline(e, units, NT, lead, step)

            @block.scalar
            def _(e):
                credits(e, s_stage, 2)

                def step(i, j, u, new, old):
                    q = j % 2
                    if new:
                        wait(e, s_red, u - 1)
                        e.wait_ge(s_proj, u + 1)
                        e.activation(sq[:, q, :], ps[:, q, :], ACT.Square).then_inc(s_sq, 1)
                    if old:
                        wait(e, s_st[q], (i * NT + (j - lead) // 2 * 2) * 8)
                        e.wait_ge(s_t, u - lead + 1)
                        e.activation(stage[:, q, :].rearrange("p (b h s) -> p h b s", b=BPT, h=REP),
                                     ps[:, 2 + q, :].rearrange("p (h b s) -> p h b s", b=BPT, h=REP),
                                     ACT.Copy).then_inc(s_stage, 1)
                    if new:
                        e.wait_ge(s_ms, u + 1)
                        e.activation(rt[:, q, :], ss[:, q, :], ACT.Sqrt).then_inc(s_rt, 1)

                pipeline(e, units, NT, lead, step)

            @block.vector
            def _(e):
                e.wait_ge(s_tab, 5)

                def step(i, j, u, new, old):
                    t, q, b = j % NT, j % 2, (j - 1) % 2
                    if new:
                        e.wait_ge(s_sq, u + 1)
                        e.tensor_reduce(ss[:, q, :], heads(sq[:, q, :]), AX.X, ALU.add).then_inc(s_red, 1)
                        e.wait_ge(s_red, u + 1)
                        e.tensor_scalar(ss[:, q, :], ss[:, q, :], 1.0 / D, EPS, ALU.mult, ALU.add).then_inc(s_ms, 1)
                    if j > 0 and (new or j == NT):
                        e.wait_ge(s_m1, u)
                        e.wait_ge(s_m2, u)
                        wait(e, s_t, u - 2)
                        e.tensor_tensor(qr[:, b, :], m1[:, b, :], m2[:, b, :], ALU.add).then_inc(s_qr, 1)
                    if new:
                        e.wait_ge(s_rt, u + 1)
                        e.reciprocal(rs[:, q, :], rt[:, q, :]).then_inc(s_rs, 1)
                        e.wait_ge(s_rs, u + 1)
                        wait(e, s_m2, u - 1)
                        e.tensor_tensor(heads(qn[:, q, :]), heads(ps[:, q, :]), spread(rs[:, q, :], 2, D),
                                        ALU.mult).then_inc(s_qn, 1)
                        e.wait_ge(s_qn, u + 1)
                        e.tensor_tensor(heads(m1[:, q, :]), heads(qn[:, q, :]), spread(ta[:, t, :], 1, REP),
                                        ALU.mult).then_inc(s_m1, 1)

                pipeline(e, units, NT, lead, step)


def project_values(nc, ps, dram, xh, xl, chunk0, chunks, v_own):
    with ExitStack() as ctx:
        w = Weights(nc, ctx, "pv", dram["wqkv"])
        stage = ctx.enter_context(nc.sbuf_tensor("pv_stage", [P, 2, 512], F32))
        s_proj, s_stage = (ctx.enter_context(nc.semaphore("pv_s_" + n)) for n in ("proj", "stage"))
        s_st = [ctx.enter_context(nc.semaphore(f"pv_s_st{q}")) for q in range(2)]
        with nc.Block() as block:
            @block.sync
            def _(e):
                w.load(e, 0, chunk0)
                for c in range(chunks):
                    if c + 1 < chunks:
                        w.load(e, c + 1, chunk0 + c + 1)
                    for t in range(NT):
                        e.wait_ge(s_stage, c * NT + t + 1)
                        e.dma_start(v_own[t * P:(t + 1) * P, c * 512:(c + 1) * 512],
                                    stage[:, t % 2, :]).then_inc(s_st[t % 2], 16)
                for q in range(2):
                    e.wait_ge(s_st[q], 16 * chunks * NT // 2)

            @block.gpsimd
            def _(e):
                for c in range(chunks):
                    for k in range(KB):
                        w.halve(e, c, k)

            @block.tensor
            def _(e):
                with e.Fori(0, chunks) as c:
                    e.wait_ge(w.s_lo, (c + 1) * KB)
                    for t in range(NT):
                        e.wait_ge(s_stage, c * NT + t - 1) if t else e.wait_ge(s_stage, c * (NT - 1))
                        w.multiply(e, ps[:, t % 2, :], xh, xl, t, c).then_inc(s_proj, 1)

            @block.scalar
            def _(e):
                with e.Fori(0, chunks) as c:
                    for t in range(NT):
                        e.wait_ge(s_st[t % 2], (c * (NT // 2) + t // 2) * 16)
                        e.wait_ge(s_proj, c * NT + t + 1)
                        e.activation(stage[:, t % 2, :], ps[:, t % 2, :], ACT.Copy).then_inc(s_stage, 1)


def projections(nc, ps, dram, x, qk_t, v_own):
    with ExitStack() as ctx:
        xh = ctx.enter_context(nc.sbuf_tensor("xh", [P, KB, T], F32R))
        xl = ctx.enter_context(nc.sbuf_tensor("xl", [P, KB, T], F32R))
        cos = ctx.enter_context(nc.sbuf_tensor("cos", [P, NT, D // 2], F32))
        sin = ctx.enter_context(nc.sbuf_tensor("sin", [P, NT, D // 2], F32))
        with nc.semaphore("xs_hi") as s_hi, nc.semaphore("xs_lo") as s_lo, nc.Block() as block:
            @block.scalar
            def _(e):
                for k in range(KB):
                    e.activation(xh[:, k, :], x[:, k, :], ACT.Copy).then_inc(s_hi, 1)

            @block.vector
            def _(e):
                for k in range(KB):
                    e.wait_ge(s_hi, k + 1)
                    e.tensor_tensor(xl[:, k, :], x[:, k, :], xh[:, k, :].bitcast(F32), ALU.subtract).then_inc(s_lo, 1)
                e.wait_ge(s_lo, KB)
        rope_angles(nc, dram, cos, sin)
        project_rope(nc, ps, dram, "pq", xh, xl, cos, sin, 0, HK, "L1_cond_q_norm_w", qk_t)
        project_rope(nc, ps, dram, "pk", xh, xl, cos, sin, HK, HK // REP, "L1_cond_k_norm_w", qk_t)
        project_values(nc, ps, dram, xh, xl, NQU, HK // REP, v_own)


def attention(nc, ps, dram, qk_t, v_own, o_t):
    UB = HK
    PER = 2 * UB
    SC = 1.0 / math.sqrt(D)
    with ExitStack() as ctx:
        sb = lambda n, s, d=F32: ctx.enter_context(nc.sbuf_tensor("at_" + n, s, d))
        sem = lambda n: ctx.enter_context(nc.semaphore("at_" + n))
        cst = sb("cst", [P, C_FREQ])
        mod = sb("mod", [P, 1])
        leni = sb("leni", [P, B], I32)
        lenf = sb("lenf", [P, B])
        page = sb("page", [P, B * KC], I32)
        pagef = sb("pagef", [P, B * KC])
        rows = sb("rows", [P, B * KC], U32)
        idx = sb("idx", [P, 2, KC], U32)
        k_raw = sb("k_raw", [P, 2, KC, HK * D])
        v_raw = sb("v_raw", [P, 2, KC, HK * D])
        v_new = sb("v_new", [S, 2, HK * D])
        qk = sb("qk", [P, 2, NQU * P])
        mask = sb("mask", [P, 2, NKEY])
        kt = sb("kt", [P, 2, LK])
        sm = sb("sm", [P, 2, NKEY])
        pr = sb("pr", [P, 4, NKEY])
        mx, nm, su, ri = (sb(n, [P, 4]) for n in ("mx", "nm", "su", "ri"))
        pt = sb("pt", [P, 2, LK])
        pt_new = sb("pt_new", [S, 2, P])
        ot = sb("ot", [P, 2, UB * P])
        s_rows = sem("rows")
        s_in, s_v, s_one, s_idx, s_ktt, s_kt, s_mask, s_s, s_max, s_nm, s_e, s_ri, s_pn, s_c, s_pt, s_pv, s_o = (
            sem(n) for n in ("in", "v", "one", "idx", "ktt", "kt", "mask", "s", "max", "nm", "e", "ri", "pn", "c",
                             "pt", "pv", "o"))
        s_passed = [sem("passed_pool"), sem("passed_vector")]
        s_k, s_vr, s_qk, s_vn, s_ot = ([sem(f"{n}{q}") for q in range(2)] for n in ("k", "vr", "qk", "vn", "ot"))
        ps_w, ps_wn, ps_k, ps_o = ps[:, 4, :], ps[0:S, 5, 0:P], ps[:, 6, :], ps[:, 7, 0:P]

        def scores(r):
            whole = ps[:, 2 * r:2 * r + 2, :].rearrange("p a b -> p (a b)")
            return whole[:, 0:NKEY], whole[:, 0:LK], whole[:, LK:NKEY]

        steps = lambda e, step: turns(e, B * UB, PER, 5, step)

        with nc.Block() as block:
            @block.sync
            def _(e):
                e.dma_start(cst[:, :], dram["cst"][:, 0:C_FREQ]).then_inc(s_in, 16)
                e.dma_start(mod[:, :], dram["cst"][:, C_MOD:C_MOD + 1], allow_slow_non_contiguous=True).then_inc(s_in, 16)
                e.dma_start(leni[:, :], bass.AP(tensor=dram["itok_B_207_1644"].tensor, offset=0, ap=[[0, P], [1, B]])).then_inc(s_in, 16)
                for q in range(BPT):
                    src = bass.AP(tensor=dram["itok_Bx16_0_63"].tensor, offset=q, ap=[[0, PSIZE], [BPT, B * KC]])
                    e.dma_start(page[q * PSIZE:(q + 1) * PSIZE, :], src, allow_slow_non_contiguous=True).then_inc(s_in, 16)

                def load_qk(b, q):
                    wait(e, s_s, (b - 1) * UB)
                    src = qk_t[bass.ds(b, 1), :, :] if not isinstance(b, int) else qk_t[b:b + 1, :, :]
                    e.dma_start(qk[:, q, :], src.rearrange("o d x -> (o d) x")).then_inc(s_qk[q], 16)

                def load_v(b, q):
                    wait(e, s_pv, (b - 1) * UB)
                    src = v_own[bass.ds(b * S, S), :] if not isinstance(b, int) else v_own[b * S:(b + 1) * S, :]
                    e.dma_start(v_new[:, q, :], src).then_inc(s_vn[q], 16)

                def store(b, q):
                    e.wait_ge(s_o, (b + 1) * UB)
                    dst = o_t[bass.ds(b, 1), :, :] if not isinstance(b, int) else o_t[b:b + 1, :, :]
                    e.dma_start(dst.rearrange("o d x -> (o d) x"), ot[:, q, :]).then_inc(s_ot[q], 16)

                load_qk(0, 0)
                load_v(0, 0)
                load_qk(1, 1)
                load_v(1, 1)
                with e.Fori(0, B // 2 - 1) as i:
                    for q in range(2):
                        load_qk(i * 2 + (q + 2), q)
                        load_v(i * 2 + (q + 2), q)
                        store(i * 2 + q, q)
                store(B - 2, 0)
                store(B - 1, 1)
                for q in range(2):
                    e.wait_ge(s_ot[q], 16 * B // 2)

            @block.gpsimd
            def _(e):
                e.memset(mask[:, :, :], 0.0).then_inc(s_one, 1)

                def gather(cache, buf, c, q, sem_q):
                    e.indirect_dma_start(out=buf[:, q, c, :], out_offset=None, in_=cache,
                                         in_offset=bass.IndirectOffsetOnAxis(ap=idx[:, q, c:c + 1], axis=0)
                                         ).then_inc(sem_q[q], 16)

                def indices(b, q):
                    e.wait_ge(s_rows, 1)
                    src = rows[:, b * KC:(b + 1) * KC] if isinstance(b, int) else rows[:, bass.ds(b * KC, KC)]
                    e.tensor_copy(idx[:, q, :], src).then_inc(s_idx, 1)

                indices(0, 0)
                e.wait_ge(s_idx, 1)
                for c in range(KC):
                    gather(dram["k_cache"], k_raw, c, 0, s_k)
                for c in range(KC):
                    gather(dram["v_cache"], v_raw, c, 0, s_vr)

                def step(i, j, u, live):
                    if live(0) and not (isinstance(i, int) and i == B // 2 - 1 and j >= UB):
                        g, q = j % UB, (j // UB + 1) % 2
                        b = i * 2 + j // UB
                        if g == 0:
                            wait_apart(e, s_passed[0], (s_ktt, b * UB))
                            indices(b + 1, q)
                            wait_apart(e, s_passed[0], (s_idx, b + 2))
                        if g == KC:
                            wait_apart(e, s_passed[0], (s_pv, b * UB))
                        if g < KC:
                            gather(dram["k_cache"], k_raw, g, q, s_k)
                        else:
                            gather(dram["v_cache"], v_raw, g - KC, q, s_vr)

                steps(e, step)

            @block.tensor
            def _(e):
                ident = cst[:, C_ID:C_ID + P]

                def step(i, j, u, live):
                    if live(0):
                        g, q = j % UB, (j // UB) % 2
                        if g == 0:
                            e.wait_ge(s_k[q], (i + j // PER) * 16 * KC + 16 * KC)
                        wait(e, s_kt, u)
                        for c in range(KC):
                            last = e.transpose(ps_k[:, c * P:(c + 1) * P], k_raw[:, q, c, g * D:(g + 1) * D], ident)
                        last.then_inc(s_ktt, 1)
                    if live(1):
                        m, jj = u - 1, j - 1
                        g, q, r = jj % UB, (jj // UB) % 2, jj % 2
                        if g == 0:
                            e.wait_ge(s_qk[q], (i + jj // PER) * 16 + 16)
                        e.wait_ge(s_kt, m + 1)
                        wait(e, s_max, m - 1)
                        _, cached, new = scores(r)
                        e.matmul(new, qk[:, q, g * P:(g + 1) * P],
                                 qk[:, q, HK * P + g * S:HK * P + (g + 1) * S], start=True, stop=True)
                        e.matmul(cached, qk[:, q, g * P:(g + 1) * P], kt[:, r, :],
                                 start=True, stop=True).then_inc(s_s, 1)
                    if live(3):
                        m, jj = u - 3, j - 3
                        r, r4 = jj % 2, jj % 4
                        e.wait_ge(s_pn, m + 1)
                        wait(e, s_pt, m)
                        for c in range(KC):
                            e.transpose(ps_w[:, c * P:(c + 1) * P], pr[:, r4, c * P:(c + 1) * P], ident)
                        e.transpose(ps_wn, pr[:, r4, LK:NKEY], ident).then_inc(s_c, 1)
                    if live(4):
                        m, jj = u - 4, j - 4
                        g, q, r = jj % UB, (jj // UB) % 2, jj % 2
                        if g == 0:
                            e.wait_ge(s_vr[q], (i + jj // PER) * 16 * KC + 16 * KC)
                            e.wait_ge(s_vn[q], (i + jj // PER) * 16 + 16)
                        e.wait_ge(s_pt, m + 1)
                        wait(e, s_o, m)
                        out = ps_o
                        for c in range(KC):
                            e.matmul(out, v_raw[:, q, c, g * D:(g + 1) * D], pt[:, r, c * P:(c + 1) * P],
                                     start=(c == 0), stop=False)
                        e.matmul(out, v_new[:, q, g * D:(g + 1) * D], pt_new[:, r, :],
                                 start=False, stop=True).then_inc(s_pv, 1)

                e.wait_ge(s_in, 16 * (3 + BPT))
                steps(e, step)

            @block.vector
            def _(e):
                line = Line(e, s_v)
                v = lambda f: line(f(e))
                e.wait_ge(s_in, 16 * (3 + BPT))
                v(lambda e: e.tensor_copy(pagef[:, :], page[:, :]))
                v(lambda e: e.tensor_scalar(pagef[:, :], pagef[:, :], float(PSIZE), mod[:, 0:1], ALU.mult, ALU.add))
                e.tensor_copy(rows[:, :], pagef[:, :]).then_inc(s_rows, 1)
                v(lambda e: e.tensor_copy(lenf[:, :], leni[:, :]))
                e.wait_ge(s_one, 1)

                def step(i, j, u, live):
                    if live(0):
                        wait(e, s_s, u - 1)
                        e.wait_ge(s_ktt, u + 1)
                        e.tensor_copy(kt[:, j % 2, :], ps_k).then_inc(s_kt, 1)
                    if live(2):
                        m, r = u - 2, (j - 2) % 4
                        e.wait_ge(s_e, m + 1)
                        e.reciprocal(ri[:, r:r + 1], su[:, r:r + 1]).then_inc(s_ri, 1)
                        e.wait_ge(s_ri, m + 1)
                        e.tensor_scalar(pr[:, r, :], pr[:, r, :], ri[:, r:r + 1], None, ALU.mult).then_inc(s_pn, 1)
                    if live(1):
                        m, jj = u - 1, j - 1
                        q, r, r4 = (jj // UB) % 2, jj % 2, jj % 4
                        if jj % UB == 0:
                            b = i * 2 + jj // UB
                            length = lenf[:, b:b + 1] if isinstance(b, int) else lenf[:, bass.ds(b, 1)]
                            e.tensor_scalar(mask[:, q, 0:LK], cst[:, C_IOTA:C_IOTA + LK], length, NEG,
                                            ALU.is_ge, ALU.mult).then_inc(s_mask, 1)
                        wait_apart(e, s_passed[1], (s_mask, i * 2 + jj // UB + 1), (s_s, m + 1), (s_e, m - 1))
                        e.tensor_tensor_reduce(out=sm[:, r, :], in0=scores(r)[0], in1=mask[:, q, :], scale=1.0,
                                               scalar=-3e38, op0=ALU.add, op1=ALU.max,
                                               accum_out=mx[:, r4:r4 + 1]).then_inc(s_max, 1)
                    if live(1):
                        e.wait_ge(s_max, u)
                        r4 = (j - 1) % 4
                        e.tensor_scalar(nm[:, r4:r4 + 1], mx[:, r4:r4 + 1], -SC, None, ALU.mult).then_inc(s_nm, 1)

                steps(e, step)

            @block.scalar
            def _(e):
                def step(i, j, u, live):
                    if live(5):
                        m, jj = u - 5, j - 5
                        g, q, r = jj % UB, (jj // UB) % 2, jj % 2
                        if g == 0:
                            wait(e, s_ot[q], (i + jj // PER) * 16)
                        e.wait_ge(s_pv, m + 1)
                        e.activation(ot[:, q, g * P:(g + 1) * P], ps_o, ACT.Copy).then_inc(s_o, 1)
                    if live(3):
                        m, r = u - 3, (j - 3) % 2
                        wait(e, s_pv, m - 1)
                        e.wait_ge(s_c, m + 1)
                        e.activation(pt[:, r, :], ps_w, ACT.Copy)
                        e.activation(pt_new[:, r, :], ps_wn, ACT.Copy).then_inc(s_pt, 1)
                    if live(1):
                        m, jj = u - 1, j - 1
                        r, r4 = jj % 2, jj % 4
                        wait(e, s_c, m - 3)
                        e.wait_ge(s_nm, m + 1)
                        e.activation(pr[:, r4, :], sm[:, r, :], ACT.Exp, bias=nm[:, r4:r4 + 1], scale=SC,
                                     accum_out=su[:, r4:r4 + 1]).then_inc(s_e, 1)

                steps(e, step)


def output_projection(nc, ps, dram, o_t, att):
    CB = T // 512
    BB = B // CB
    PER = 2 * CB
    with ExitStack() as ctx:
        sb = lambda n, s, d=F32: ctx.enter_context(nc.sbuf_tensor("op_" + n, s, d))
        sem = lambda n: ctx.enter_context(nc.semaphore("op_" + n))
        w_raw = sb("w_raw", [P, REP, L])
        w_hi, w_lo = (sb(n, [P, 2, REP, L], F32R) for n in ("w_hi", "w_lo"))
        o_raw = sb("o_raw", [P, 2, BB, P])
        o_hi, o_lo = (sb(n, [P, 2, BB, P], F32R) for n in ("o_hi", "o_lo"))
        s_passed, s_w, s_whi, s_wlo, s_ohi, s_olo, s_mm, s_acc = (
            sem(n) for n in ("passed", "w", "whi", "wlo", "ohi", "olo", "mm", "acc"))
        s_o = [sem("o0"), sem("o1")]
        with nc.Block() as block:
            @block.sync
            def _(e):
                def load_w(g):
                    wait(e, s_wlo, g * REP)
                    src = dram["wo"][bass.ds(g * REP, REP), :, :] if not isinstance(g, int) else dram["wo"][g * REP:(g + 1) * REP, :, :]
                    e.dma_start(w_raw[:, :, :], src.rearrange("h d o -> d h o")).then_inc(s_w, 16)

                def load_o(g, u, c, q):
                    wait(e, s_olo, u - 1)
                    cols = slice(g * P, (g + 1) * P) if isinstance(g, int) else bass.ds(g * P, P)
                    e.dma_start(o_raw[:, q, :, :], o_t[c * BB:(c + 1) * BB, :, cols].rearrange("b d x -> d b x")).then_inc(s_o[q], 16)

                def turn(g):
                    for c in range(CB):
                        load_o(g, g * CB + c, c, c % 2)
                        if c == 1 and not (isinstance(g, int) and g == HK - 1):
                            load_w(g + 1)

                load_w(0)
                turn(0)
                with e.Fori(1, HK - 1) as g:
                    turn(g)
                turn(HK - 1)

            @block.gpsimd
            def _(e):
                def halve(g, par):
                    for r in range(REP):
                        if r == 0:
                            wait_apart(e, s_passed, (s_w, g * 16 + 16), (s_mm, (g - 1) * CB))
                        e.tensor_copy(w_hi[:, par, r, :], w_raw[:, r, :]).then_inc(s_whi, 1)
                        wait_apart(e, s_passed, (s_whi, g * REP + r + 1))
                        e.tensor_tensor(w_lo[:, par, r, :], w_raw[:, r, :], w_hi[:, par, r, :].bitcast(F32),
                                        ALU.subtract).then_inc(s_wlo, 1)
                halve(0, 0)
                halve(1, 1)
                with e.Fori(1, HK // 2) as i:
                    for q in range(2):
                        halve(i * 2 + q, q)

            @block.scalar
            def _(e):
                def step(i, j, u, live):
                    if live(0):
                        q = j % 2
                        wait(e, s_mm, u - 1)
                        e.wait_ge(s_o[q], (i * (PER // 2) + j // 2) * 16 + 16)
                        e.activation(o_hi[:, q, :, :], o_raw[:, q, :, :], ACT.Copy).then_inc(s_ohi, 1)

                turns(e, HK * CB, PER, 1, step)

            @block.vector
            def _(e):
                e.memset(att[:, :, :], 0.0).then_inc(s_acc, 1)

                def step(i, j, u, live):
                    if live(0):
                        q = j % 2
                        e.wait_ge(s_ohi, u + 1)
                        wait(e, s_mm, u - 1)
                        e.tensor_tensor(o_lo[:, q, :, :], o_raw[:, q, :, :], o_hi[:, q, :, :].bitcast(F32),
                                        ALU.subtract).then_inc(s_olo, 1)
                    if live(1):
                        m, jj = u - 1, j - 1
                        c, bank = jj % CB, (jj % 2) * KB
                        e.wait_ge(s_mm, m + 1)
                        wait(e, s_acc, m * KB + 1)
                        for ob in range(KB):
                            a = att[:, ob, c * 512:(c + 1) * 512]
                            e.tensor_tensor(a, a, ps[:, bank + ob, :], ALU.add).then_inc(s_acc, 1)

                turns(e, HK * CB, PER, 1, step)

            @block.tensor
            def _(e):
                def step(i, j, u, live):
                    if not live(0):
                        return
                    c, q, par, bank = j % CB, j % 2, (j // CB) % 2, (j % 2) * KB
                    if c == 0:
                        e.wait_ge(s_wlo, (i * 2 + j // CB + 1) * REP)
                    e.wait_ge(s_olo, u + 1)
                    wait(e, s_acc, (u - 1) * KB + 1)
                    for ob in range(KB):
                        for r in range(REP):
                            cols, x = slice(ob * P, (ob + 1) * P), slice(r * S, (r + 1) * S)
                            out = ps[:, bank + ob, :]
                            e.matmul(out, w_hi[:, par, r, cols], o_hi[:, q, :, x], start=(r == 0), stop=False)
                            e.matmul(out, w_hi[:, par, r, cols], o_lo[:, q, :, x], start=False, stop=False)
                            last = e.matmul(out, w_lo[:, par, r, cols], o_hi[:, q, :, x], start=False, stop=(r == REP - 1))
                    last.then_inc(s_mm, 1)

                turns(e, HK * CB, PER, 1, step)


def build(nc, dram, out_t, stop=9):
    taps = nc.dram_tensor("taps", [S, KPW], F32).ap()
    with ExitStack() as ctx:
        ps = ctx.enter_context(nc.psum_tensor("ps", [P, 8, 512], F32))
        s4d_taps(nc, ps, dram, taps)
        with nc.sbuf_tensor("x_sb", [P, KB, T], F32) as x_t:
            with nc.sbuf_tensor("y_sb", [P, KB, T], F32) as y_t:
                convolve(nc, ps, dram, taps, y_t)
                with nc.semaphore("s_load") as s_load, nc.Block() as block:
                    @block.sync
                    def _(e):
                        for k in range(KB):
                            e.dma_start(x_t[:, k, :], dram["x_t"][k * P:(k + 1) * P, :]).then_inc(s_load, 16)
                        e.wait_ge(s_load, 16 * KB)
                ffn(nc, ps, dram, ("w0", "b0", "g0", "a0", "lb0"), "0", y_t, x_t, 1.0)
            if stop == 2:
                with nc.semaphore("s_dbg") as s_dbg, nc.Block() as block:
                    @block.sync
                    def _(e):
                        for k in range(KB):
                            e.dma_start(out_t[k * P:(k + 1) * P, :], x_t[:, k, :]).then_inc(s_dbg, 16)
                        e.wait_ge(s_dbg, 16 * KB)
                return
            qk_t = nc.dram_tensor("qk_t", [B, P, NQU * P], F32).ap()
            v_own = nc.dram_tensor("v_own", [T, HK * D], F32).ap()
            projections(nc, ps, dram, x_t, qk_t, v_own)
            if stop == 3:
                with nc.semaphore("s_dbg") as s_dbg, nc.Block() as block:
                    @block.sync
                    def _(e):
                        e.dma_start(dram["dbg_qk"], qk_t).then_inc(s_dbg, 16)
                        e.dma_start(dram["dbg_v"], v_own).then_inc(s_dbg, 16)
                        e.wait_ge(s_dbg, 32)
                return
            o_t = nc.dram_tensor("o_t", [B, P, HK * P], F32).ap()
            attention(nc, ps, dram, qk_t, v_own, o_t)
            with nc.sbuf_tensor("att", [P, KB, T], F32) as att:
                output_projection(nc, ps, dram, o_t, att)
                ffn(nc, ps, dram, ("w1", "b1", "g1", "a1", "lb1"), "1", att, x_t, 2.0, out=out_t)




def layouts(i):
    c = lambda a: np.ascontiguousarray(a)
    x = i["x"]
    out = {"cst": constants()}
    out["x_t"] = c(x.transpose(2, 0, 1).reshape(L, T))
    out["x_rev"] = c(x.transpose(2, 1, 0).reshape(KB, P, S, B)[:, ::-1].reshape(L, S, B))
    for n in ("itok_B_8_3872", "itok_Bx16_0_63", "itok_B_207_1644", "L0_cond_log_dt", "L0_cond_D",
              "L1_cond_q_norm_w", "L1_cond_k_norm_w"):
        out[n] = c(i[n])
    out["log_a"] = c(i["L0_cond_log_A_real"].reshape(HP, P).T)
    out["a_imag"] = c(i["L0_cond_A_imag"].reshape(HP, P).T)
    out["c"] = c(i["L0_cond_C"].reshape(HP, P, 2).transpose(1, 0, 2))
    w = np.concatenate([i["L1_cond_Wq"], i["L1_cond_Wk"], i["L1_cond_Wv"]])
    out["wqkv"] = c(w.reshape(NQU + HK // REP, 512, L).transpose(0, 2, 1))
    out["wo"] = c(i["L1_cond_Wo"].T.reshape(HQ, D, L))
    out["k_cache"] = c(i["L1_cond_k_cache"].reshape(PAGES * PSIZE, HK * D))
    out["v_cache"] = c(i["L1_cond_v_cache"].reshape(PAGES * PSIZE, HK * D))
    for n, p, g, a, b in (("0", "L0_ffn_", "W_gate", "A", "B"), ("1", "L1_ffn_", "W_router", "A_stack", "B_stack")):
        out["w" + n] = c(i[p + "W_base"].T)
        out["b" + n] = c(i[p + "b_base"].reshape(KB, P).T)
        out["g" + n] = c(i[p + g].T)
        out["a" + n] = c(i[p + a].reshape(E * R, L).T)
        out["lb" + n] = c(i[p + b].transpose(0, 2, 1).reshape(E * R, L))
    return out


def kernel(**inputs):
    import concourse.bacc as bacc
    from concourse.bass_utils import run_bass_kernel_spmd

    arrays = layouts({k: np.asarray(v) for k, v in inputs.items()})
    nc = bacc.Bacc("TRN2", target_bir_lowering=False, num_devices=1)
    dram = {k: nc.dram_tensor(k, v.shape, mybir.dt.from_np(v.dtype), kind="ExternalInput").ap() for k, v in arrays.items()}
    out_t = nc.dram_tensor("out_t", [L, T], F32, kind="ExternalOutput").ap()
    build(nc, dram, out_t)
    r = run_bass_kernel_spmd(nc, [arrays], core_ids=[0])
    return np.ascontiguousarray(r.results[0]["out_t"].reshape(L, B, S).transpose(1, 2, 0))
```

```python
from contextlib import ExitStack
import math

import numpy as np

import concourse.bass as bass
from concourse import mybir

F32 = mybir.dt.float32
F32R = mybir.dt.float32r
I32 = mybir.dt.int32
U32 = mybir.dt.uint32
ALU = mybir.AluOpType
ACT = mybir.ActivationFunctionType
AX = mybir.AxisListType

P = 128
B, S, L = 64, 32, 512
T = B * S
KB = L // P
NS = 64
HP = S // 2
E, R = 8, 16
HQ, HK, D = 32, 8, 128
REP = HQ // HK
PAGES, PSIZE, NPP = 64, 32, 16
LK = NPP * PSIZE
NKEY = LK + S
NT = T // P
BPT = P // S
KC = LK // P
PPT = P // PSIZE
KT = PAGES // PPT
NQU = HK + HK // REP
THETA, EPS = 10000.0, 1e-6
NEG = -1e30
KPW = P + L

MAGIC = 1.5 * 2.0 ** 23
LN2_HI, LN2_LO = 0.693359375, -2.12194440e-4
TWO_PI_1 = 6.28125
TWO_PI_2 = float(np.float32(math.floor((2 * math.pi - TWO_PI_1) * 2 ** 20) / 2 ** 20))
TWO_PI_3 = 2 * math.pi - TWO_PI_1 - TWO_PI_2
PI_SAFE = 3.1415925

NMUL = 48
C_ID = 0
C_IOTA = C_ID + P
C_EXPAND = C_IOTA + LK
C_FREQ = C_EXPAND + P
C_MUL = C_FREQ + D // 2
C_DESC = C_MUL + NMUL
C_ROW = C_DESC + E
C_REV = C_ROW + KB
C_MOD = C_REV + KB
C_ALL = C_MOD + 1


def constants():
    c = np.zeros((P, C_ALL), np.float32)
    c[:, C_ID:C_ID + P] = np.eye(P)
    c[:, C_IOTA:C_IOTA + LK] = np.arange(LK)
    for e in range(E):
        c[e, C_EXPAND + e * R:C_EXPAND + (e + 1) * R] = 1.0
    exponents = np.arange(0, D, 2, dtype=np.float32) / np.float32(D)
    c[:, C_FREQ:C_FREQ + D // 2] = np.float32(1.0) / np.power(np.float32(THETA), exponents)
    c[:, C_MUL:C_MUL + 32] = np.arange(32)
    c[:, C_MUL + 32:C_MUL + 48] = 32 * np.arange(16)
    c[:, C_DESC:C_DESC + E] = E - np.arange(E)
    for k in range(KB):
        c[:, C_ROW + k] = k * P + np.arange(P)
        c[:, C_REV + k] = k * P + P - 1 - np.arange(P)
    c[:, C_MOD] = np.arange(P) % S
    return c


class Line:

    def __init__(self, eng, sem):
        self.eng, self.sem, self.n = eng, sem, 0

    def __call__(self, ins):
        ins.then_inc(self.sem, 1)
        self.n += 1
        self.eng.wait_ge(self.sem, self.n)


def credits(eng, sem, n):
    for _ in range(n):
        eng.nop().then_inc(sem, 1)


def spread(ap, axis, n):
    ap = ap.unsqueeze(axis)
    shape = list(ap.shape)
    shape[axis] = n
    return ap.to_broadcast(shape)


def exp_exact(v, x, out, t, k, p):
    v(lambda e: e.tensor_scalar(x, x, 88.0, -87.0, ALU.min, ALU.max))
    v(lambda e: e.tensor_scalar(t, x, 1.0 / math.log(2.0), MAGIC + 127.0, ALU.mult, ALU.add))
    v(lambda e: e.tensor_scalar(k, t, MAGIC + 127.0, None, ALU.subtract))
    v(lambda e: e.scalar_tensor_tensor(out=x, in0=k, scalar=-LN2_HI, in1=x, op0=ALU.mult, op1=ALU.add))
    v(lambda e: e.scalar_tensor_tensor(out=x, in0=k, scalar=-LN2_LO, in1=x, op0=ALU.mult, op1=ALU.add))
    v(lambda e: e.tensor_scalar(p, x, 1.0 / 5040.0, None, ALU.mult))
    for c in (1 / 720, 1 / 120, 1 / 24, 1 / 6, 0.5, 1.0):
        v(lambda e, c=c: e.scalar_tensor_tensor(out=p, in0=p, scalar=c, in1=x, op0=ALU.add, op1=ALU.mult))
    v(lambda e: e.tensor_scalar(k.bitcast(I32), t.bitcast(I32), 23, None, ALU.logical_shift_left))
    v(lambda e: e.scalar_tensor_tensor(out=out, in0=p, scalar=1.0, in1=k, op0=ALU.add, op1=ALU.mult))


def reduce_angle(v, f, t, sin_arg, cos_arg, u=None):
    v(lambda e: e.tensor_scalar(t, f, 1.0 / (2 * math.pi), MAGIC, ALU.mult, ALU.add))
    v(lambda e: e.tensor_scalar(t, t, MAGIC, None, ALU.subtract))
    for part in (TWO_PI_1, TWO_PI_2, TWO_PI_3):
        if u is None:
            v(lambda e: e.scalar_tensor_tensor(out=f, in0=t, scalar=-part, in1=f, op0=ALU.mult, op1=ALU.add))
        else:
            v(lambda e: e.tensor_scalar(u, t, part, None, ALU.mult))
            v(lambda e: e.tensor_tensor(f, f, u, ALU.subtract))
    v(lambda e: e.tensor_scalar(sin_arg, f, PI_SAFE, -PI_SAFE, ALU.min, ALU.max))
    v(lambda e: e.tensor_scalar(f, sin_arg, 0.0, math.pi / 2, ALU.min, ALU.add))
    v(lambda e: e.tensor_scalar(cos_arg, sin_arg, 0.0, None, ALU.max))
    v(lambda e: e.tensor_tensor(cos_arg, f, cos_arg, ALU.subtract))


def s4d_taps(nc, ps, dram, taps, cst, um, mrow, k_t):
    with ExitStack() as ctx:
        sb = lambda n, s, d=F32: ctx.enter_context(nc.sbuf_tensor("s4_" + n, s, d))
        sem = lambda n: ctx.enter_context(nc.semaphore("s4_" + n))
        TB = 4
        k_in = sb("k_in", [P, TB, HK * D])
        k_out = sb("k_out", [P, TB, PPT, HK, PSIZE])
        s_kt, s_kc = sem("kt"), sem("kc")
        s_ki, s_ko = ([sem(f"{n}{q}") for q in range(TB)] for n in ("ki", "ko"))
        leni = sb("leni", [P, B], I32)
        lenf = sb("lenf", [P, B])
        mrev = sb("mrev", [P, KB, B])
        raw = sb("raw", [P, 2, HP])
        ex = sb("ex", [P, 2, HP])
        ai = sb("ai", [P, HP])
        cc = sb("cc", [P, HP, 2])
        dvec = sb("dvec", [1, S])
        small = sb("small", [P, 12, HP])
        shape = [P, HP, NMUL]
        arg, mag, t1, t2, t3, ang, sa, ca, sn, cs, er, ei = (
            sb(n, shape) for n in ("arg", "mag", "t1", "t2", "t3", "ang", "sa", "ca", "sn", "cs", "er", "ei"))
        ur, ui, ut = (sb(n, [P, HP, 16]) for n in ("ur", "ui", "ut"))
        kev = sb("kev", [16, HP, 2, 32])
        zeros = sb("zeros", [S, P])
        s_in, s_v, s_sin, s_u, s_k, s_ev, s_out, s_len, s_x, s_g = (
            sem(n) for n in ("in", "v", "sin", "u", "k", "ev", "out", "len", "x", "g"))
        done = {}
        mul = cst[:, C_MUL:C_MUL + NMUL]
        with nc.Block() as block:
            @block.sync
            def _(e):
                e.dma_start(cst[:, :], dram["cst"]).then_inc(s_in, 16)
                for half in range(2):
                    src = bass.AP(tensor=dram["L0_cond_log_dt"].tensor, offset=half, ap=[[0, NS], [2, HP]])
                    e.dma_start(raw[half * NS:(half + 1) * NS, 0, :], src, allow_slow_non_contiguous=True).then_inc(s_in, 16)
                e.dma_start(raw[:, 1, :], dram["log_a"]).then_inc(s_in, 16)
                e.dma_start(ai[:, :], dram["a_imag"]).then_inc(s_in, 16)
                e.dma_start(cc[:, :, :], dram["c"]).then_inc(s_in, 16)
                e.dma_start(dvec[:, :], dram["L0_cond_D"].rearrange("(o h) -> o h", o=1)).then_inc(s_in, 16)
                src = bass.AP(tensor=dram["itok_B_8_3872"].tensor, offset=0, ap=[[0, P], [1, B]])
                e.dma_start(leni[:, :], src).then_inc(s_len, 16)
                for k in range(KB):
                    e.dma_start(um[:, k, :, :], dram["x_rev"][k * P:(k + 1) * P, :, :]).then_inc(s_x, 16)
                for n in range(TB):
                    e.dma_start(k_in[:, n, :], dram["k_cache"][n * P:(n + 1) * P, :]).then_inc(s_ki[n], 16)
                k_rows = k_t.rearrange("(t n d) x -> t d n x", n=PPT, d=P)

                def store(t, q):
                    e.wait_ge(s_kc, (t + 1) * 2 + 2)
                    t = slice(t, t + 1) if isinstance(t, int) else bass.ds(t, 1)
                    e.dma_start(k_rows[t, :, :, :].rearrange("o d n x -> (o d) n x"),
                                k_out[:, q, :, :, :].rearrange("p n g k -> p n (g k)")).then_inc(s_ko[q], 16)

                with e.Fori(0, KT // TB - 1) as i:
                    for q in range(TB):
                        store(i * TB + q, q)
                        e.dma_start(k_in[:, q, :], dram["k_cache"][bass.ds((i * TB + q + TB) * P, P), :]).then_inc(s_ki[q], 16)
                for q in range(TB):
                    store(KT - TB + q, q)
                for q in range(TB):
                    e.wait_ge(s_ko[q], 16 * KT // TB)
                e.wait_ge(s_ev, 1)
                e.dma_start(taps[:, P:KPW].rearrange("h (a b) -> a h b", b=32),
                            kev[:, :, :, :].rearrange("a i t b -> a (i t) b")).then_inc(s_out, 16)
                e.dma_start(taps[:, 0:P], zeros[:, :]).then_inc(s_out, 16)
                e.wait_ge(s_out, 32)

            @block.vector
            def _(e):
                line = Line(e, s_v)
                v = lambda f: line(f(e))
                v(lambda e: e.memset(zeros[:, :], 0.0))
                e.wait_ge(s_in, 16 * 7)
                flat = lambda x: x.rearrange("p a b -> p (a b)")
                w = [small[:, i, :] for i in range(12)]
                tmp = small[:, 6:12, :]
                exp_exact(v, flat(raw[:, :, :]), flat(ex[:, :, :]), flat(tmp[:, 0:2, :]),
                          flat(tmp[:, 2:4, :]), flat(tmp[:, 4:6, :]))
                ar, dar, dai = w[0], w[1], w[2]
                v(lambda e: e.tensor_scalar(ar, ex[:, 1, :], -1.0, None, ALU.mult))
                v(lambda e: e.tensor_tensor(dar, ar, ex[:, 0, :], ALU.mult))
                v(lambda e: e.tensor_tensor(dai, ai[:, :], ex[:, 0, :], ALU.mult))
                mulb = spread(mul, 1, HP)
                v(lambda e: e.tensor_tensor(ang[:, :, :], spread(dai, 2, NMUL), mulb, ALU.mult))
                reduce_angle(v, flat(ang[:, :, :]), flat(t1[:, :, :]), flat(sa[:, :, :]), flat(ca[:, :, :]))
                done["angles"] = line.n
                v(lambda e: e.tensor_tensor(arg[:, :, :], spread(dar, 2, NMUL), mulb, ALU.mult))
                exp_exact(v, flat(arg[:, :, :]), flat(mag[:, :, :]), flat(t1[:, :, :]), flat(t2[:, :, :]), flat(t3[:, :, :]))
                e.wait_ge(s_sin, 2)
                v(lambda e: e.tensor_tensor(er[:, :, :], mag[:, :, :], cs[:, :, :], ALU.mult))
                v(lambda e: e.tensor_tensor(ei[:, :, :], mag[:, :, :], sn[:, :, :], ALU.mult))
                zr, zi, nr, ni, t, u = w[3], ei[:, :, 1], w[4], w[5], w[6], w[7]
                cr, ci = cc[:, :, 0], cc[:, :, 1]
                v(lambda e: e.tensor_scalar(zr, er[:, :, 1], 1.0, None, ALU.subtract))
                v(lambda e: e.tensor_tensor(nr, cr, zr, ALU.mult))
                v(lambda e: e.tensor_tensor(t, ci, zi, ALU.mult))
                v(lambda e: e.tensor_tensor(nr, nr, t, ALU.subtract))
                v(lambda e: e.tensor_tensor(ni, cr, zi, ALU.mult))
                v(lambda e: e.tensor_tensor(t, ci, zr, ALU.mult))
                v(lambda e: e.tensor_tensor(ni, ni, t, ALU.add))
                sr, si, den = w[8], w[9], w[10]
                v(lambda e: e.tensor_tensor(sr, nr, ar, ALU.mult))
                v(lambda e: e.tensor_tensor(t, ni, ai[:, :], ALU.mult))
                v(lambda e: e.tensor_tensor(sr, sr, t, ALU.add))
                v(lambda e: e.tensor_tensor(si, ni, ar, ALU.mult))
                v(lambda e: e.tensor_tensor(t, nr, ai[:, :], ALU.mult))
                v(lambda e: e.tensor_tensor(si, si, t, ALU.subtract))
                v(lambda e: e.tensor_tensor(den, ar, ar, ALU.mult))
                v(lambda e: e.tensor_tensor(t, ai[:, :], ai[:, :], ALU.mult))
                v(lambda e: e.tensor_tensor(den, den, t, ALU.add))
                v(lambda e: e.reciprocal(u, den))
                v(lambda e: e.scalar_tensor_tensor(out=sr, in0=sr, scalar=2.0, in1=u, op0=ALU.mult, op1=ALU.mult))
                v(lambda e: e.scalar_tensor_tensor(out=si, in0=si, scalar=2.0, in1=u, op0=ALU.mult, op1=ALU.mult))
                ear, eai = er[:, :, 32:48], ei[:, :, 32:48]
                srb, sib = spread(sr, 2, 16), spread(si, 2, 16)
                v(lambda e: e.tensor_tensor(ur[:, :, :], srb, ear, ALU.mult))
                v(lambda e: e.tensor_tensor(ut[:, :, :], sib, eai, ALU.mult))
                v(lambda e: e.tensor_tensor(ur[:, :, :], ur[:, :, :], ut[:, :, :], ALU.subtract))
                v(lambda e: e.tensor_tensor(ui[:, :, :], srb, eai, ALU.mult))
                v(lambda e: e.tensor_tensor(ut[:, :, :], sib, ear, ALU.mult))
                e.scalar_tensor_tensor(out=ui[:, :, :], in0=ui[:, :, :], scalar=-1.0, in1=ut[:, :, :],
                                       op0=ALU.mult, op1=ALU.subtract).then_inc(s_u, 1)
                e.wait_ge(s_k, 1)
                for half in range(2):
                    v(lambda e: e.tensor_copy(kev[:, :, half, :], ps[0:16, half, :].rearrange("a (i b) -> a i b", b=32)))
                d = kev[0:1, :, :, 0:1].rearrange("a i t b -> a (i t b)")
                e.tensor_tensor(d, d, dvec[:, :], ALU.add).then_inc(s_ev, 1)

            @block.gpsimd
            def _(e):
                line = Line(e, s_g)
                v = lambda f: line(f(e))
                e.wait_ge(s_len, 16)
                e.wait_ge(s_in, 16 * 7)
                v(lambda e: e.tensor_copy(lenf[:, :], leni[:, :]))
                for k in range(KB):
                    v(lambda e: e.tensor_scalar(mrev[:, k, :], lenf[:, :], cst[:, C_REV + k:C_REV + k + 1], None, ALU.is_gt))
                    v(lambda e: e.tensor_scalar(mrow[:, k, :], lenf[:, :], cst[:, C_ROW + k:C_ROW + k + 1], None, ALU.is_gt))
                e.wait_ge(s_x, 16 * KB)
                for k in range(KB):
                    e.tensor_tensor(um[:, k, :, :], um[:, k, :, :], spread(mrev[:, k, :], 1, S), ALU.mult)

            @block.scalar
            def _(e):
                e.wait_ge(s_v, done["angles"])
                e.activation(sn[:, :, :], sa[:, :, :], ACT.Sin).then_inc(s_sin, 1)
                e.activation(cs[:, :, :], ca[:, :, :], ACT.Sin).then_inc(s_sin, 1)
                credits(e, s_kc, 2)
                with e.Fori(0, KT // TB) as i:
                    for q in range(TB):
                        e.wait_ge(s_ko[q], i * 16)
                        for half in range(2):
                            heads = slice(half * HK // 2, (half + 1) * HK // 2)
                            e.wait_ge(s_kt, (i * TB + q) * 2 + half + 1)
                            e.activation(k_out[:, q, :, heads, :].rearrange("p n g k -> p g n k"),
                                         ps[:, 4 + 2 * (q % 2) + half, :].rearrange("p (g n k) -> p g n k", n=PPT, k=PSIZE),
                                         ACT.Copy).then_inc(s_kc, 1)

            @block.tensor
            def _(e):
                e.wait_ge(s_in, 16 * 7)

                def turn_keys(first, end):
                    with e.Fori(first, end) as i:
                        for q in range(TB):
                            e.wait_ge(s_ki[q], i * 16 + 16)
                            e.wait_ge(s_kc, (i * TB + q) * 2)
                            for half in range(2):
                                for g in range(HK // 2):
                                    x = slice((half * HK // 2 + g) * D, (half * HK // 2 + g + 1) * D)
                                    last = e.transpose(ps[:, 4 + 2 * (q % 2) + half, g * P:(g + 1) * P], k_in[:, q, x],
                                                       cst[:, C_ID:C_ID + P])
                                last.then_inc(s_kt, 1)

                turn_keys(0, 2)
                e.wait_ge(s_u, 1)
                for half in range(2):
                    rows = slice(half * NS, (half + 1) * NS)
                    for i in range(HP):
                        out = ps[0:16, half, i * 32:(i + 1) * 32]
                        e.matmul(out, ur[rows, i, :], er[rows, i, 0:32], start=True, stop=False)
                        last = e.matmul(out, ui[rows, i, :], ei[rows, i, 0:32], start=False, stop=True)
                last.then_inc(s_k, 1)
                turn_keys(2, KT // TB)


def convolve(nc, ps, dram, taps, cst, um, mrow, y_t, cos, sin):
    TB, YB, H = 8, 4, D // 2
    with ExitStack() as ctx:
        sb = lambda n, s, d=F32: ctx.enter_context(nc.sbuf_tensor("cv_" + n, s, d))
        sem = lambda n: ctx.enter_context(nc.semaphore("cv_" + n))
        toe = sb("toe", [P, TB, L])
        leni = sb("leni", [P, NT], I32)
        pos = sb("pos", [P, NT])
        f, t = sb("f", [P, NT, H]), sb("t", [P, NT, H])
        s_y, s_mm, s_len, s_g, s_sin = (sem(n) for n in ("y", "mm", "len", "g", "sin"))
        s_toe = [sem(f"toe{q}") for q in range(TB)]
        y_v = y_t[:, :, :].rearrange("p k (b h) -> p k b h", h=S)
        flat = lambda x: x[:, :, :].rearrange("p a b -> p (a b)")
        done = {}

        def load(e, h, q):
            src = bass.AP(tensor=taps.tensor, offset=h * KPW + 1, ap=[[1, P], [1, L]])
            e.dma_start(toe[:, q, :], src).then_inc(s_toe[q], 16)

        with nc.Block() as block:
            @block.sync
            def _(e):
                for q in range(TB):
                    load(e, q, q)
                for q in range(BPT):
                    src = bass.AP(tensor=dram["itok_B_207_1644"].tensor, offset=q, ap=[[0, S], [BPT, NT]])
                    e.dma_start(leni[q * S:(q + 1) * S, :], src, allow_slow_non_contiguous=True).then_inc(s_len, 16)
                with e.Fori(0, S // TB - 1) as i:
                    for q in range(TB):
                        e.wait_ge(s_mm, i * TB + q + 1)
                        load(e, i * TB + q + TB, q)

            @block.vector
            def _(e):
                credits(e, s_y, YB)
                with e.Fori(0, S // TB) as i:
                    for q in range(TB):
                        e.wait_ge(s_mm, i * TB + q + 1)
                        e.tensor_tensor(y_v[:, :, :, bass.ds(i * TB + q, 1)].rearrange("p k b o -> p k (b o)"),
                                        ps[:, q % YB, 0:KB * B].rearrange("p (k b) -> p k b", k=KB),
                                        mrow[:, :, :], ALU.mult).then_inc(s_y, 1)

            @block.tensor
            def _(e):
                with e.Fori(0, S // TB) as i:
                    for q in range(TB):
                        e.wait_ge(s_toe[q], i * 16 + 16)
                        e.wait_ge(s_y, i * TB + q + 1)
                        for d in range(KB):
                            last = e.matmul(ps[:, q % YB, d * B:KB * B], toe[:, q, d * P:(d + 1) * P],
                                            um[:, 0:KB - d, bass.ds(i * TB + q, 1), :].rearrange("p k o b -> p k (o b)"),
                                            start=(d == 0), stop=(d == KB - 1))
                        last.then_inc(s_mm, 1)

            @block.gpsimd
            def _(e):
                line = Line(e, s_g)
                v = lambda g: line(g(e))
                e.wait_ge(s_len, 16 * BPT)
                v(lambda e: e.tensor_copy(pos[:, :], leni[:, :]))
                v(lambda e: e.tensor_scalar(pos[:, :], pos[:, :], cst[:, C_MOD:C_MOD + 1], None, ALU.add))
                v(lambda e: e.tensor_tensor(f[:, :, :], spread(pos[:, :], 2, H),
                                            spread(cst[:, C_FREQ:C_FREQ + H], 1, NT), ALU.mult))
                reduce_angle(v, flat(f), flat(t), flat(sin), flat(cos), u=flat(cos))
                done["angles"] = line.n

            @block.scalar
            def _(e):
                e.wait_ge(s_g, done["angles"])
                e.activation(sin[:, :, :], sin[:, :, :], ACT.Sin).then_inc(s_sin, 1)
                e.activation(cos[:, :, :], cos[:, :, :], ACT.Sin).then_inc(s_sin, 1)
                e.wait_ge(s_sin, 2)


def rope_tables(e, sem, cos, sin, nw, ta, tb):
    H = D // 2
    for kind in range(2):
        rows = slice(kind * NT, (kind + 1) * NT)
        w1, w2 = spread(nw[:, kind, 0:H], 1, NT), spread(nw[:, kind, H:D], 1, NT)
        e.tensor_tensor(ta[:, rows, 0:H], cos[:, :, :], w1, ALU.mult)
        e.tensor_tensor(ta[:, rows, H:D], cos[:, :, :], w2, ALU.mult)
        e.tensor_tensor(tb[:, rows, H:D], sin[:, :, :], w1, ALU.mult)
        e.tensor_tensor(tb[:, rows, 0:H], sin[:, :, :], w2, ALU.mult).then_inc(sem, 1)
    e.wait_ge(sem, 2)
    e.tensor_scalar(tb[:, :, 0:H], tb[:, :, 0:H], -1.0, None, ALU.mult)


def ffn(nc, ps, dram, names, tag, act, src, out, scaling, cst, halves=None, tables=None):
    w_n, b_n, g_n, a_n, lb_n = names
    NB = T // 512
    with ExitStack() as ctx:
        sb = lambda n, s, d=F32: ctx.enter_context(nc.sbuf_tensor(f"f{tag}_{n}", s, d))
        sem = lambda n: ctx.enter_context(nc.semaphore(f"f{tag}_{n}"))
        w = sb("w", [P, KB, L])
        a = sb("a", [P, KB, E * R])
        g = sb("g", [P, KB, E])
        lb = sb("lb", [E * R, L])
        bias = sb("bias", [P, KB])
        resid = sb("resid", [P, 2, KB, 512])
        lgt = sb("lgt", [E, T])
        lg, eq, one1, one2, l2 = (sb(n, [P, NT, E]) for n in ("lg", "eq", "one1", "one2", "l2"))
        m1, m2, fm, d, e2, p1, p2 = (sb(n, [P, NT]) for n in ("m1", "m2", "fm", "d", "e2", "p1", "p2"))
        route = sb("route", [P, NT, E])
        route_t = sb("route_t", [E, 2, 512])
        wexp = sb("wexp", [E * R, 512])
        hw = sb("hw", [E * R, 512])
        s_g, s_in, s_lt, s_lc, s_lg, s_v, s_e2, s_rt, s_rte, s_we, s_wx, s_h, s_hw, s_mm, s_ev, s_hi, s_lo, s_tab = (
            sem(n) for n in ("g", "in", "lt", "lc", "lg", "v", "e2", "rt", "rte", "we", "wx", "h", "hw", "mm", "ev",
                             "hi", "lo", "tab"))
        s_res, s_out = ([sem(f"{n}{q}") for q in range(2)] for n in ("res", "out"))
        done = {}
        if tables:
            nw = sb("nw", [P, 2, D])
            s_nw = sem("nw")
        with nc.Block() as block:
            @block.sync
            def _(e):
                e.dma_start(g[:, :, :], dram[g_n].rearrange("(k p) e -> p k e", p=P)).then_inc(s_g, 16)
                e.dma_start(bias[:, :], dram[b_n]).then_inc(s_in, 16)
                e.dma_start(a[:, :, :], dram[a_n].rearrange("(k p) r -> p k r", p=P)).then_inc(s_in, 16)
                e.dma_start(w[:, :, :], dram[w_n].rearrange("(k p) o -> p k o", p=P)).then_inc(s_in, 16)
                e.dma_start(lb[:, :], dram[lb_n]).then_inc(s_in, 16)
                if tables:
                    for kind, name in enumerate(("L1_cond_q_norm_w", "L1_cond_k_norm_w")):
                        row = bass.AP(tensor=dram[name].tensor, offset=0, ap=[[0, P], [1, D]])
                        e.dma_start(nw[:, kind, :], row).then_inc(s_nw, 16)

                def load(i):
                    cols = slice(i * 512, (i + 1) * 512)
                    e.dma_start(resid[:, i % 2, :, :], src[:, cols].rearrange("(k p) n -> p k n", p=P)).then_inc(s_res[i % 2], 16)

                load(0)
                load(1)
                for i in range(NB):
                    e.wait_ge(s_ev, KB * (i + 2))
                    cols = slice(i * 512, (i + 1) * 512)
                    e.dma_start(out[:, cols].rearrange("(k p) n -> p k n", p=P), resid[:, i % 2, :, :]).then_inc(s_out[i % 2], 16)
                    if i + 2 < NB:
                        e.wait_ge(s_out[i % 2], (i // 2 + 1) * 16)
                        if halves:
                            e.wait_ge(s_lo, KB * (i + 1))
                        load(i + 2)
                for q in range(2):
                    e.wait_ge(s_out[q], 16 * NB // 2)

            if tables:
                @block.gpsimd
                def _(e):
                    e.wait_ge(s_nw, 32)
                    rope_tables(e, s_tab, tables[0], tables[1], nw, tables[2], tables[3])

            @block.vector
            def _(e):
                line = Line(e, s_v)
                v = lambda f: line(f(e))
                e.wait_ge(s_lg, 1)
                v(lambda e: e.tensor_copy(lg[:, :, :], ps[:, 0, 0:NT * E].rearrange("p (t e) -> p t e", e=E)))
                desc = spread(cst[:, C_DESC:C_DESC + E], 1, NT)

                def pick(logits, m, one):
                    v(lambda e: e.tensor_reduce(m[:, :], logits[:, :, :], AX.X, ALU.max))
                    v(lambda e: e.tensor_tensor(eq[:, :, :], logits[:, :, :], spread(m[:, :], 2, E), ALU.is_equal))
                    v(lambda e: e.tensor_tensor(eq[:, :, :], eq[:, :, :], desc, ALU.mult))
                    v(lambda e: e.tensor_reduce(fm[:, :], eq[:, :, :], AX.X, ALU.max))
                    v(lambda e: e.tensor_tensor(one[:, :, :], desc, spread(fm[:, :], 2, E), ALU.is_equal))

                pick(lg, m1, one1)
                v(lambda e: e.scalar_tensor_tensor(out=l2[:, :, :], in0=one1[:, :, :], scalar=-3e38, in1=lg[:, :, :],
                                                   op0=ALU.mult, op1=ALU.add))
                pick(l2, m2, one2)
                v(lambda e: e.tensor_tensor(d[:, :], m2[:, :], m1[:, :], ALU.subtract))
                done["gap"] = line.n
                e.wait_ge(s_e2, 1)
                v(lambda e: e.tensor_scalar(p1[:, :], e2[:, :], 1.0, None, ALU.add))
                v(lambda e: e.reciprocal(p1[:, :], p1[:, :]))
                v(lambda e: e.tensor_tensor(p2[:, :], e2[:, :], p1[:, :], ALU.mult))
                v(lambda e: e.tensor_tensor(one1[:, :, :], one1[:, :, :], spread(p1[:, :], 2, E), ALU.mult))
                v(lambda e: e.tensor_tensor(one2[:, :, :], one2[:, :, :], spread(p2[:, :], 2, E), ALU.mult))
                v(lambda e: e.tensor_tensor(route[:, :, :], one1[:, :, :], one2[:, :, :], ALU.add))
                done["route"] = line.n
                credits(e, s_ev, KB)
                e.wait_ge(s_in, 16 * 4)
                for i in range(NB):
                    e.wait_ge(s_wx, i + 1)
                    e.wait_ge(s_h, i + 1)
                    e.scalar_tensor_tensor(out=hw[:, :], in0=ps[:, 6, :], scalar=scaling, in1=wexp[:, :],
                                           op0=ALU.mult, op1=ALU.mult).then_inc(s_hw, 1)
                    e.wait_ge(s_res[i % 2], (i // 2 + 1) * 16)
                    for ob in range(KB):
                        r = resid[:, i % 2, ob, :]
                        e.wait_ge(s_mm, i * KB + ob + 1)
                        e.scalar_tensor_tensor(out=r, in0=ps[:, 1 + ob, :], scalar=bias[:, ob:ob + 1], in1=r,
                                               op0=ALU.add, op1=ALU.add).then_inc(s_ev, 1)
                    if halves:
                        for ob in range(KB):
                            cols = slice(i * 512, (i + 1) * 512)
                            e.wait_ge(s_hi, i * KB + ob + 1)
                            e.tensor_tensor(halves[1][:, ob, cols], resid[:, i % 2, ob, :],
                                            halves[0][:, ob, cols].bitcast(F32), ALU.subtract).then_inc(s_lo, 1)

            @block.scalar
            def _(e):
                for i in range(NB):
                    e.wait_ge(s_lt, i + 1)
                    e.activation(lgt[:, i * 512:(i + 1) * 512], ps[0:E, 4 + i, :], ACT.Copy).then_inc(s_lc, 1)
                e.wait_ge(s_v, done["gap"])
                e.activation(e2[:, :], d[:, :], ACT.Exp).then_inc(s_e2, 1)
                for i in range(NB):
                    e.wait_ge(s_rt, i + 1)
                    e.activation(route_t[:, i % 2, :], ps[0:E, 7, :], ACT.Copy).then_inc(s_rte, 1)
                    wait(e, s_hw, i)
                    e.wait_ge(s_we, i + 1)
                    e.activation(wexp[:, :], ps[:, 5, :], ACT.Copy).then_inc(s_wx, 1)
                    if halves:
                        for ob in range(KB):
                            e.wait_ge(s_ev, KB * (i + 1) + ob + 1)
                            e.activation(halves[0][:, ob, i * 512:(i + 1) * 512], resid[:, i % 2, ob, :],
                                         ACT.Copy).then_inc(s_hi, 1)

            @block.tensor
            def _(e):
                e.wait_ge(s_g, 16)
                for i in range(NB):
                    for k in range(KB):
                        last = e.matmul(ps[0:E, 4 + i, :], g[:, k, :], act[:, k, i * 512:(i + 1) * 512],
                                        start=(k == 0), stop=(k == KB - 1))
                    last.then_inc(s_lt, 1)
                e.wait_ge(s_lc, NB)
                for t in range(NT):
                    last = e.transpose(ps[:, 0, t * E:(t + 1) * E], lgt[:, t * P:(t + 1) * P], cst[0:E, C_ID:C_ID + E])
                last.then_inc(s_lg, 1)
                e.wait_ge(s_in, 16 * 4)

                def turn_weights(i):
                    e.wait_ge(s_v, done["route"])
                    wait(e, s_rte, i)
                    for t in range(4):
                        last = e.transpose(ps[0:E, 7, t * P:(t + 1) * P], route[:, i * 4 + t, :], cst[:, C_ID:C_ID + P])
                    last.then_inc(s_rt, 1)

                def expand(i):
                    wait(e, s_wx, i)
                    e.wait_ge(s_rte, i + 1)
                    e.matmul(ps[:, 5, :], cst[0:E, C_EXPAND:C_EXPAND + P], route_t[:, i % 2, :],
                             start=True, stop=True).then_inc(s_we, 1)

                for i in range(NB):
                    cols = slice(i * 512, (i + 1) * 512)
                    if i > 0:
                        turn_weights(i)
                    wait(e, s_hw, i)
                    for k in range(KB):
                        last = e.matmul(ps[:, 6, :], a[:, k, :], act[:, k, cols], start=(k == 0), stop=(k == KB - 1))
                    last.then_inc(s_h, 1)
                    if i > 0:
                        expand(i)
                    for ob in range(KB):
                        e.wait_ge(s_ev, i * KB + ob + 1)
                        for k in range(KB):
                            e.matmul(ps[:, 1 + ob, :], w[:, k, ob * P:(ob + 1) * P], act[:, k, cols],
                                     start=(k == 0), stop=False)
                    if i == 0:
                        turn_weights(i)
                        expand(i)
                    e.wait_ge(s_hw, i + 1)
                    for ob in range(KB):
                        e.matmul(ps[:, 1 + ob, :], lb[:, ob * P:(ob + 1) * P], hw[:, :],
                                 start=False, stop=True).then_inc(s_mm, 1)


def wait(eng, sem, value):
    if not isinstance(value, int) or value > 0:
        eng.wait_ge(sem, value)


def wait_apart(eng, sem_passed, *waits):
    for sem, v in waits:
        wait(eng, sem, v)
    eng.sem_inc(sem_passed, 1)


def turns(eng, units, per, lead, step):
    for u in range(lead):
        step(0, u, u, lambda off: u - off >= 0)
    with eng.Fori(0, units // per - 1) as i:
        for j in range(lead, per + lead):
            step(i, j, i * per + j, lambda off: True)
    i = units // per - 1
    for j in range(lead, per + lead):
        step(i, j, i * per + j, lambda off: j - off < per)


class Weights:

    def __init__(self, nc, ctx, tag, src):
        self.src = src
        self.raw = ctx.enter_context(nc.sbuf_tensor(f"{tag}_raw", [P, KB, 512], F32))
        self.hi = ctx.enter_context(nc.sbuf_tensor(f"{tag}_hi", [P, 2 * KB, 512], F32R))
        self.lo = ctx.enter_context(nc.sbuf_tensor(f"{tag}_lo", [P, 2 * KB, 512], F32R))
        self.s_raw, self.s_hi, self.s_lo, self.s_passed = (
            ctx.enter_context(nc.semaphore(f"{tag}_{n}")) for n in ("s_raw", "s_hi", "s_lo", "s_passed"))

    def load(self, e, c, chunk):
        wait(e, self.s_lo, c * KB)
        src = self.src[bass.ds(chunk, 1), :, :] if not isinstance(chunk, int) else self.src[chunk:chunk + 1, :, :]
        e.dma_start(self.raw[:, :, :], src.rearrange("o (k p) n -> p (o k) n", p=P)).then_inc(self.s_raw, 16)

    def pick(self, part, c, k):
        row = (c % 2) * KB + k
        row = slice(row, row + 1) if isinstance(row, int) else bass.ds(row, 1)
        return part[:, row, :].rearrange("p o n -> p (o n)")

    def high(self, e, c, k):
        e.wait_ge(self.s_raw, c * 16 + 16)
        e.activation(self.pick(self.hi, c, k), self.raw[:, k, :], ACT.Copy).then_inc(self.s_hi, 1)

    def low(self, e, c, k):
        e.wait_ge(self.s_hi, c * KB + k + 1)
        e.tensor_tensor(self.pick(self.lo, c, k), self.raw[:, k, :], self.pick(self.hi, c, k).bitcast(F32),
                        ALU.subtract).then_inc(self.s_lo, 1)

    def multiply(self, e, out, xh, xl, t, c):
        par = (c % 2) * KB
        for k in range(KB):
            w = slice(par + k, par + k + 1) if isinstance(par, int) else bass.ds(par + k, 1)
            hi = self.hi[:, w, :].rearrange("p o n -> p (o n)")
            lo = self.lo[:, w, :].rearrange("p o n -> p (o n)")
            cols = slice(t * P, (t + 1) * P)
            e.matmul(out, xh[:, k, cols], hi, start=(k == 0), stop=False)
            e.matmul(out, xh[:, k, cols], lo, start=False, stop=False)
            last = e.matmul(out, xl[:, k, cols], hi, start=False, stop=(k == KB - 1))
        return last


def project(nc, ps, dram, cst, xh, xl, ta, tb, qk_t, v_own):
    H = D // 2
    with ExitStack() as ctx:
        sb = lambda n, s, d=F32: ctx.enter_context(nc.sbuf_tensor("pr_" + n, s, d))
        sem = lambda n: ctx.enter_context(nc.semaphore("pr_s_" + n))
        w = Weights(nc, ctx, "pr", dram["wqkv"])
        sq = sb("sq", [P, 512])
        qn, m1, m2, qr, stage = (sb(n, [P, 2, 512]) for n in ("qn", "m1", "m2", "qr", "stage"))
        ss, rt, rs = (sb(n, [P, 4, REP]) for n in ("ss", "rt", "rs"))
        s_proj, s_red, s_ms, s_rt, s_rs, s_qn, s_m1, s_m2, s_qr, s_t, s_stage = (
            sem(n) for n in ("proj", "red", "ms", "rt", "rs", "qn", "m1", "m2", "qr", "t", "stage"))
        s_st = [sem("st0"), sem("st1")]
        heads = lambda a: a.rearrange("p (h x) -> p h x", h=REP)
        chunk = lambda i, j: i + j // NT
        steps = lambda e, step: turns(e, NQU * NT, NT, 6, step)
        chunks = NQU + HK // REP
        values = [(c, t, c * NT + t) for c in range(NQU, chunks) for t in range(NT)]

        def table(tab, i, jj, cols):
            c, t = chunk(i, jj), jj % NT
            row = (c // HK) * NT + t
            row = slice(row, row + 1) if isinstance(row, int) else bass.ds(row, 1)
            return tab[:, row, cols].to_broadcast([P, REP, cols.stop - cols.start])

        with nc.Block() as block:
            @block.sync
            def _(e):
                w.load(e, 0, 0)

                def step(i, j, u, live):
                    if live(0) and j % NT == 0:
                        w.load(e, chunk(i, j) + 1, chunk(i, j) + 1)
                    if live(6):
                        jj = j - 6
                        t, q, c = jj % NT, jj % 2, chunk(i, jj)
                        e.wait_ge(s_stage, u - 6 + 1)
                        cols = bass.ds(c * P, P) if not isinstance(c, int) else slice(c * P, (c + 1) * P)
                        e.dma_start(qk_t[t * BPT:(t + 1) * BPT, :, cols].rearrange("b d x -> d b x"),
                                    stage[:, q, :].rearrange("p (b x) -> p b x", b=BPT)).then_inc(s_st[q], 16)

                steps(e, step)
                for c, t, n in values:
                    if t == 0 and c + 1 < chunks:
                        w.load(e, c + 1, c + 1)
                    e.wait_ge(s_stage, n + 1)
                    e.dma_start(v_own[t * P:(t + 1) * P, (c - NQU) * 512:(c - NQU + 1) * 512],
                                stage[:, t % 2, :]).then_inc(s_st[t % 2], 16)
                for q in range(2):
                    e.wait_ge(s_st[q], 16 * chunks * NT // 2)

            @block.scalar
            def _(e):
                for k in range(KB):
                    w.high(e, 0, k)

                def step(i, j, u, live):
                    if live(1):
                        m, r = u - 1, (j - 1) % 4
                        wait(e, s_ms, m)
                        e.wait_ge(s_proj, m + 1)
                        for h in range(REP):
                            ins = e.activation(sq[:, h * D:(h + 1) * D], ps[:, r, h * D:(h + 1) * D], ACT.Square, accum_out=ss[:, r, h:h + 1])
                        ins.then_inc(s_red, 1)
                    if live(6):
                        m, q, n = u - 6, (j - 6) % 2, (j - 6) // 2
                        wait(e, s_st[q], (i * (NT // 2) + n) * 16)
                        e.wait_ge(s_t, m + 1)
                        e.activation(stage[:, q, :].rearrange("p (b h s) -> p h b s", b=BPT, h=REP),
                                     ps[:, 4 + q, :].rearrange("p (h b s) -> p h b s", b=BPT, h=REP),
                                     ACT.Copy).then_inc(s_stage, 1)
                    if live(2):
                        m, r = u - 2, (j - 2) % 4
                        e.wait_ge(s_ms, m + 1)
                        e.activation(rt[:, r, :], ss[:, r, :], ACT.Sqrt).then_inc(s_rt, 1)
                    t = j % NT
                    if t % 3 == 1 and t // 3 < KB and live(0):
                        w.high(e, chunk(i, j) + 1, t // 3)

                steps(e, step)
                for c, t, n in values:
                    if t < KB and c + 1 < chunks:
                        w.high(e, c + 1, t)
                    e.wait_ge(s_st[t % 2], (n // 2) * 16)
                    e.wait_ge(s_proj, n + 1)
                    e.activation(stage[:, t % 2, :], ps[:, t % 4, :], ACT.Copy).then_inc(s_stage, 1)

            @block.vector
            def _(e):
                for k in range(KB):
                    w.low(e, 0, k)

                def step(i, j, u, live):
                    if live(2):
                        m, r = u - 2, (j - 2) % 4
                        e.wait_ge(s_red, m + 1)
                        e.tensor_scalar(ss[:, r, :], ss[:, r, :], 1.0 / D, EPS, ALU.mult, ALU.add).then_inc(s_ms, 1)
                    if live(3):
                        m, q, r = u - 3, (j - 3) % 2, (j - 3) % 4
                        e.wait_ge(s_rt, m + 1)
                        e.reciprocal(rs[:, r, :], rt[:, r, :]).then_inc(s_rs, 1)
                        e.wait_ge(s_rs, m + 1)
                        wait(e, s_m2, m - 1)
                        e.tensor_tensor(heads(qn[:, q, :]), heads(ps[:, r, :]), spread(rs[:, r, :], 2, D),
                                        ALU.mult).then_inc(s_qn, 1)
                    if live(4):
                        m, q = u - 4, (j - 4) % 2
                        e.wait_ge(s_m1, m + 1)
                        e.wait_ge(s_m2, m + 1)
                        wait(e, s_t, m - 1)
                        e.tensor_tensor(qr[:, q, :], m1[:, q, :], m2[:, q, :], ALU.add).then_inc(s_qr, 1)
                    if live(3):
                        m, q = u - 3, (j - 3) % 2
                        e.wait_ge(s_qn, m + 1)
                        e.tensor_tensor(heads(m1[:, q, :]), heads(qn[:, q, :]), table(ta, i, j - 3, slice(0, D)),
                                        ALU.mult).then_inc(s_m1, 1)
                    t = j % NT
                    if t % 3 == 2 and t // 3 < KB and live(0):
                        w.low(e, chunk(i, j) + 1, t // 3)

                steps(e, step)
                for c in range(NQU + 1, chunks):
                    for k in range(KB):
                        w.low(e, c, k)

            @block.gpsimd
            def _(e):
                def step(i, j, u, live):
                    if live(3):
                        m, q = u - 3, (j - 3) % 2
                        wait_apart(e, w.s_passed, (s_qr, m - 1), (s_qn, m + 1))
                        for half in range(2):
                            a, b = slice(half * H, half * H + H), slice(H - half * H, D - half * H)
                            ins = e.tensor_tensor(heads(m2[:, q, :])[:, :, a], heads(qn[:, q, :])[:, :, b],
                                                  table(tb, i, j - 3, a), ALU.mult)
                        ins.then_inc(s_m2, 1)

                steps(e, step)

            @block.tensor
            def _(e):
                def step(i, j, u, live):
                    if live(0):
                        t, r = j % NT, j % 4
                        if t == 0:
                            e.wait_ge(w.s_lo, (chunk(i, j) + 1) * KB)
                        wait(e, s_qn, u - 3)
                        w.multiply(e, ps[:, r, :], xh, xl, t, chunk(i, j)).then_inc(s_proj, 1)
                    if live(5):
                        m, q = u - 5, (j - 5) % 2
                        wait(e, s_stage, m - 1)
                        e.wait_ge(s_qr, m + 1)
                        for h in range(REP):
                            last = e.transpose(ps[:, 4 + q, h * P:(h + 1) * P], qr[:, q, h * D:(h + 1) * D], cst[:, C_ID:C_ID + P])
                        last.then_inc(s_t, 1)

                steps(e, step)
                e.wait_ge(s_qn, NQU * NT)
                for c, t, n in values:
                    if t == 0:
                        e.wait_ge(w.s_lo, (c + 1) * KB)
                    e.wait_ge(s_stage, n - 3)
                    w.multiply(e, ps[:, t % 4, :], xh, xl, t, c).then_inc(s_proj, 1)


def attention(nc, ps, dram, cst, k_t, qk_t, v_own, o_t):
    UB = HK
    PER = 2 * UB
    OWN = 2
    SC = 1.0 / math.sqrt(D)
    with ExitStack() as ctx:
        sb = lambda n, s, d=F32: ctx.enter_context(nc.sbuf_tensor("at_" + n, s, d))
        sem = lambda n: ctx.enter_context(nc.semaphore("at_" + n))
        leni = sb("leni", [P, B], I32)
        lenf = sb("lenf", [P, B])
        pagef = sb("pagef", [P, B * KC])
        rows = sb("rows", [P, B * KC], U32)
        page = sb("page", [P, B * NPP], I32)
        pagef_k = sb("pagef_k", [P, B * NPP])
        rows_k = sb("rows_k", [P, B * NPP], U32)
        idx = sb("idx", [P, 2, KC], U32)
        idx_k = sb("idx_k", [P, 2, NPP], U32)
        kt = sb("kt", [P, 2, NPP, HK * PSIZE])
        v_raw = sb("v_raw", [P, 2, KC, HK * D])
        v_new = sb("v_new", [S, 2, HK * D])
        qk = sb("qk", [P, 2, NQU * P])
        k_hi, k_lo = (sb(n, [P, 4, LK], F32R) for n in ("k_hi", "k_lo"))
        q_hi, q_lo = (sb(n, [P, 4, P], F32R) for n in ("q_hi", "q_lo"))
        mask = sb("mask", [P, 2, NKEY])
        sm = sb("sm", [P, 2, NKEY])
        pr = sb("pr", [P, 4, NKEY])
        mx, nm, su, ri = (sb(n, [P, 4]) for n in ("mx", "nm", "su", "ri"))
        pt = sb("pt", [P, 2, LK])
        pt_new = sb("pt_new", [S, 2, P])
        ot = sb("ot", [P, 2, UB * P])
        s_rows = sem("rows")
        s_in, s_v, s_one, s_hi, s_lo, s_idx, s_mask, s_s, s_max, s_nm, s_e, s_ri, s_pn, s_c, s_pt, s_pv, s_o = (
            sem(n) for n in ("in", "v", "one", "hi", "lo", "idx", "mask", "s", "max", "nm", "e", "ri", "pn", "c",
                             "pt", "pv", "o"))
        s_passed = [sem("passed_pool"), sem("passed_vector")]
        s_k, s_kp, s_vr, s_qk, s_vn, s_ot = (
            [sem(f"{n}{q}") for q in range(2)] for n in ("k", "kp", "vr", "qk", "vn", "ot"))
        ps_w, ps_wn, ps_o = ps[:, 4, :], ps[0:S, 5, 0:P], ps[:, 7, 0:P]

        def scores(r):
            whole = ps[:, 2 * r:2 * r + 2, :].rearrange("p a b -> p (a b)")
            return whole[:, 0:NKEY], whole[:, 0:LK], whole[:, LK:NKEY]

        by_page = lambda x: x.rearrange("p (n k) -> p n k", k=PSIZE)
        steps = lambda e, step: turns(e, B * UB, PER, 6, step)

        with nc.Block() as block:
            @block.sync
            def _(e):
                e.dma_start(leni[:, :], bass.AP(tensor=dram["itok_B_207_1644"].tensor, offset=0, ap=[[0, P], [1, B]])).then_inc(s_in, 16)
                src = bass.AP(tensor=dram["itok_Bx16_0_63"].tensor, offset=0, ap=[[0, P], [1, B * NPP]])
                e.dma_start(page[:, :], src).then_inc(s_in, 16)

                def load_qk(b, q):
                    wait(e, s_s, (b - 1) * UB)
                    src = qk_t[bass.ds(b, 1), :, :] if not isinstance(b, int) else qk_t[b:b + 1, :, :]
                    e.dma_start(qk[:, q, :], src.rearrange("o d x -> (o d) x")).then_inc(s_qk[q], 16)

                def load_v(b, q):
                    wait(e, s_pv, (b - 1) * UB)
                    src = v_own[bass.ds(b * S, S), :] if not isinstance(b, int) else v_own[b * S:(b + 1) * S, :]
                    e.dma_start(v_new[:, q, :], src).then_inc(s_vn[q], 16)

                def store(b, q):
                    e.wait_ge(s_o, (b + 1) * UB)
                    dst = o_t[bass.ds(b, 1), :, :] if not isinstance(b, int) else o_t[b:b + 1, :, :]
                    e.dma_start(dst.rearrange("o d x -> (o d) x"), ot[:, q, :]).then_inc(s_ot[q], 16)

                def load_pages(b, q):
                    wait(e, s_lo, (b - 1) * UB)
                    for n in range(OWN):
                        at = b * NPP + n
                        at = slice(at, at + 1) if isinstance(at, int) else bass.ds(at, 1)
                        number = e.value_load(page[0:1, at], min_val=0, max_val=PAGES - 1)
                        e.dma_start(kt[:, q, n, :], k_t[bass.ds(number * P, P), :]).then_inc(s_kp[q], 16)

                load_qk(0, 0)
                e.wait_ge(s_in, 32)
                load_pages(0, 0)
                load_v(0, 0)
                load_qk(1, 1)
                load_pages(1, 1)
                load_v(1, 1)
                with e.Fori(0, B // 2 - 1) as i:
                    for q in range(2):
                        load_qk(i * 2 + (q + 2), q)
                        load_pages(i * 2 + (q + 2), q)
                        load_v(i * 2 + (q + 2), q)
                        store(i * 2 + q, q)
                store(B - 2, 0)
                store(B - 1, 1)
                for q in range(2):
                    e.wait_ge(s_ot[q], 16 * B // 2)

            @block.gpsimd
            def _(e):
                e.memset(mask[:, :, :], 0.0).then_inc(s_one, 1)

                def gather(cache, out, index, sem_q):
                    e.indirect_dma_start(out=out, out_offset=None, in_=cache,
                                         in_offset=bass.IndirectOffsetOnAxis(ap=index, axis=0)).then_inc(sem_q, 16)

                def gather_keys(n, q):
                    gather(k_t, kt[:, q, n, :], idx_k[:, q, n:n + 1], s_k[q])

                def gather_values(c, q):
                    gather(dram["v_cache"], v_raw[:, q, c, :], idx[:, q, c:c + 1], s_vr[q])

                def indices(b, q):
                    cut = lambda x, n: x[:, b * n:(b + 1) * n] if isinstance(b, int) else x[:, bass.ds(b * n, n)]
                    e.tensor_copy(idx_k[:, q, :], cut(rows_k, NPP)).then_inc(s_idx, 1)
                    e.tensor_copy(idx[:, q, :], cut(rows, KC)).then_inc(s_idx, 1)

                e.wait_ge(s_rows, 2)
                indices(0, 0)
                e.wait_ge(s_idx, 2)
                for n in range(OWN, NPP):
                    gather_keys(n, 0)
                for c in range(KC):
                    gather_values(c, 0)

                def step(i, j, u, live):
                    if live(0) and not (isinstance(i, int) and i == B // 2 - 1 and j >= UB):
                        g, q = j % UB, (j // UB + 1) % 2
                        b = i * 2 + j // UB
                        if g == 0:
                            wait_apart(e, s_passed[0], (s_lo, b * UB))
                            indices(b + 1, q)
                            wait_apart(e, s_passed[0], (s_idx, b * 2 + 4))
                        for n in range(OWN + g * 3, min(OWN + g * 3 + 3, NPP)):
                            gather_keys(n, q)
                        if g == UB - 2:
                            wait_apart(e, s_passed[0], (s_pv, b * UB))
                        if g >= UB - 2:
                            for c in range(KC // 2):
                                gather_values((g - (UB - 2)) * KC // 2 + c, q)

                steps(e, step)

            @block.tensor
            def _(e):
                ident = cst[:, C_ID:C_ID + P]

                def step(i, j, u, live):
                    if live(2):
                        m, jj = u - 2, j - 2
                        g, q, r = jj % UB, (jj // UB) % 2, jj % 2
                        e.wait_ge(s_lo, m + 1)
                        wait(e, s_max, m - 1)
                        _, cached, new = scores(r)
                        e.matmul(new, qk[:, q, g * P:(g + 1) * P],
                                 qk[:, q, HK * P + g * S:HK * P + (g + 1) * S], start=True, stop=True)
                        e.matmul(cached, q_hi[:, jj % 4, :], k_hi[:, jj % 4, :], start=True, stop=False)
                        e.matmul(cached, q_hi[:, jj % 4, :], k_lo[:, jj % 4, :], start=False, stop=False)
                        e.matmul(cached, q_lo[:, jj % 4, :], k_hi[:, jj % 4, :], start=False, stop=True).then_inc(s_s, 1)
                    if live(4):
                        m, jj = u - 4, j - 4
                        r, r4 = jj % 2, jj % 4
                        e.wait_ge(s_pn, m + 1)
                        wait(e, s_pt, m)
                        for c in range(KC):
                            e.transpose(ps_w[:, c * P:(c + 1) * P], pr[:, r4, c * P:(c + 1) * P], ident)
                        e.transpose(ps_wn, pr[:, r4, LK:NKEY], ident).then_inc(s_c, 1)
                    if live(5):
                        m, jj = u - 5, j - 5
                        g, q, r = jj % UB, (jj // UB) % 2, jj % 2
                        if g == 0:
                            e.wait_ge(s_vr[q], (i + jj // PER) * 16 * KC + 16 * KC)
                            e.wait_ge(s_vn[q], (i + jj // PER) * 16 + 16)
                        e.wait_ge(s_pt, m + 1)
                        wait(e, s_o, m)
                        out = ps_o
                        for c in range(KC):
                            e.matmul(out, v_raw[:, q, c, g * D:(g + 1) * D], pt[:, r, c * P:(c + 1) * P],
                                     start=(c == 0), stop=False)
                        e.matmul(out, v_new[:, q, g * D:(g + 1) * D], pt_new[:, r, :],
                                 start=False, stop=True).then_inc(s_pv, 1)

                steps(e, step)

            @block.vector
            def _(e):
                line = Line(e, s_v)
                v = lambda f: line(f(e))
                e.wait_ge(s_in, 32)
                for q in range(PPT):
                    part = slice(q * PSIZE, (q + 1) * PSIZE)
                    pages = page[part, :].rearrange("p (x f) -> p x f", f=PPT)[:, :, q:q + 1].rearrange("p x f -> p (x f)")
                    v(lambda e, part=part, pages=pages: e.tensor_copy(pagef[part, :], pages))
                v(lambda e: e.tensor_scalar(pagef[:, :], pagef[:, :], float(PSIZE), cst[:, C_MOD:C_MOD + 1], ALU.mult, ALU.add))
                e.tensor_copy(rows[:, :], pagef[:, :]).then_inc(s_rows, 1)
                v(lambda e: e.tensor_copy(pagef_k[:, :], page[:, :]))
                v(lambda e: e.tensor_scalar(pagef_k[:, :], pagef_k[:, :], float(P), cst[:, C_ROW:C_ROW + 1], ALU.mult, ALU.add))
                e.tensor_copy(rows_k[:, :], pagef_k[:, :]).then_inc(s_rows, 1)
                v(lambda e: e.tensor_copy(lenf[:, :], leni[:, :]))
                e.wait_ge(s_one, 1)

                def step(i, j, u, live):
                    if live(2):
                        m, jj = u - 2, j - 2
                        q, r, r4 = (jj // UB) % 2, jj % 2, jj % 4
                        if jj % UB == 0:
                            b = i * 2 + jj // UB
                            length = lenf[:, b:b + 1] if isinstance(b, int) else lenf[:, bass.ds(b, 1)]
                            e.tensor_scalar(mask[:, q, 0:LK], cst[:, C_IOTA:C_IOTA + LK], length, NEG,
                                            ALU.is_ge, ALU.mult).then_inc(s_mask, 1)
                        wait_apart(e, s_passed[1], (s_mask, i * 2 + jj // UB + 1), (s_s, m + 1), (s_e, m - 1))
                        e.tensor_tensor_reduce(out=sm[:, r, :], in0=scores(r)[0], in1=mask[:, q, :], scale=1.0,
                                               scalar=-3e38, op0=ALU.add, op1=ALU.max,
                                               accum_out=mx[:, r4:r4 + 1]).then_inc(s_max, 1)
                        e.wait_ge(s_max, m + 1)
                        e.tensor_scalar(nm[:, r4:r4 + 1], mx[:, r4:r4 + 1], -SC, None, ALU.mult).then_inc(s_nm, 1)
                    if live(3):
                        m, r = u - 3, (j - 3) % 4
                        e.wait_ge(s_e, m + 1)
                        e.reciprocal(ri[:, r:r + 1], su[:, r:r + 1]).then_inc(s_ri, 1)
                        e.wait_ge(s_ri, m + 1)
                        e.tensor_scalar(pr[:, r, :], pr[:, r, :], ri[:, r:r + 1], None, ALU.mult).then_inc(s_pn, 1)
                    if live(0):
                        g, q, r = j % UB, (j // UB) % 2, j % 4
                        e.wait_ge(s_hi, u + 1)
                        wait(e, s_s, u - 3)
                        e.tensor_tensor(q_lo[:, r, :], qk[:, q, g * P:(g + 1) * P], q_hi[:, r, :].bitcast(F32), ALU.subtract)
                        e.tensor_tensor(by_page(k_lo[:, r, :]), kt[:, q, :, g * PSIZE:(g + 1) * PSIZE],
                                        by_page(k_hi[:, r, :]).bitcast(F32), ALU.subtract).then_inc(s_lo, 1)

                steps(e, step)

            @block.scalar
            def _(e):
                def step(i, j, u, live):
                    if live(6):
                        m, jj = u - 6, j - 6
                        g, q, r = jj % UB, (jj // UB) % 2, jj % 2
                        if g == 0:
                            wait(e, s_ot[q], (i + jj // PER) * 16)
                        e.wait_ge(s_pv, m + 1)
                        e.activation(ot[:, q, g * P:(g + 1) * P], ps_o, ACT.Copy).then_inc(s_o, 1)
                    if live(0):
                        g, q, r = j % UB, (j // UB) % 2, j % 4
                        if g == 0:
                            e.wait_ge(s_qk[q], (i + j // PER) * 16 + 16)
                            e.wait_ge(s_k[q], (i + j // PER + 1) * 16 * (NPP - OWN))
                            e.wait_ge(s_kp[q], (i + j // PER + 1) * 16 * OWN)
                        wait(e, s_s, u - 3)
                        e.activation(q_hi[:, r, :], qk[:, q, g * P:(g + 1) * P], ACT.Copy)
                        e.activation(by_page(k_hi[:, r, :]), kt[:, q, :, g * PSIZE:(g + 1) * PSIZE], ACT.Copy).then_inc(s_hi, 1)
                    if live(4):
                        m, r = u - 4, (j - 4) % 2
                        wait(e, s_pv, m - 1)
                        e.wait_ge(s_c, m + 1)
                        e.activation(pt[:, r, :], ps_w, ACT.Copy)
                        e.activation(pt_new[:, r, :], ps_wn, ACT.Copy).then_inc(s_pt, 1)
                    if live(2):
                        m, jj = u - 2, j - 2
                        r, r4 = jj % 2, jj % 4
                        wait(e, s_c, m - 3)
                        e.wait_ge(s_nm, m + 1)
                        e.activation(pr[:, r4, :], sm[:, r, :], ACT.Exp, bias=nm[:, r4:r4 + 1], scale=SC,
                                     accum_out=su[:, r4:r4 + 1]).then_inc(s_e, 1)

                steps(e, step)


def output_projection(nc, ps, dram, o_t, att):
    CB = T // 512
    BB = B // CB
    PER = 2 * CB
    with ExitStack() as ctx:
        sb = lambda n, s, d=F32: ctx.enter_context(nc.sbuf_tensor("op_" + n, s, d))
        sem = lambda n: ctx.enter_context(nc.semaphore("op_" + n))
        w_raw = sb("w_raw", [P, REP, L])
        w_hi, w_lo = (sb(n, [P, 2, REP, L], F32R) for n in ("w_hi", "w_lo"))
        o_raw = sb("o_raw", [P, 2, BB, P])
        o_hi, o_lo = (sb(n, [P, 2, BB, P], F32R) for n in ("o_hi", "o_lo"))
        s_passed, s_w, s_whi, s_wlo, s_ohi, s_olo, s_mm, s_acc = (
            sem(n) for n in ("passed", "w", "whi", "wlo", "ohi", "olo", "mm", "acc"))
        s_o = [sem("o0"), sem("o1")]
        with nc.Block() as block:
            @block.sync
            def _(e):
                def load_w(g):
                    wait(e, s_wlo, g * REP)
                    src = dram["wo"][bass.ds(g * REP, REP), :, :] if not isinstance(g, int) else dram["wo"][g * REP:(g + 1) * REP, :, :]
                    e.dma_start(w_raw[:, :, :], src.rearrange("h d o -> d h o")).then_inc(s_w, 16)

                def load_o(g, u, c, q):
                    wait(e, s_olo, u - 1)
                    cols = slice(g * P, (g + 1) * P) if isinstance(g, int) else bass.ds(g * P, P)
                    e.dma_start(o_raw[:, q, :, :], o_t[c * BB:(c + 1) * BB, :, cols].rearrange("b d x -> d b x")).then_inc(s_o[q], 16)

                def turn(g):
                    for c in range(CB):
                        load_o(g, g * CB + c, c, c % 2)
                        if c == 1 and not (isinstance(g, int) and g == HK - 1):
                            load_w(g + 1)

                load_w(0)
                turn(0)
                with e.Fori(1, HK - 1) as g:
                    turn(g)
                turn(HK - 1)

            @block.gpsimd
            def _(e):
                def halve(g, par):
                    for r in range(REP):
                        if r == 0:
                            wait_apart(e, s_passed, (s_w, g * 16 + 16), (s_mm, (g - 1) * CB))
                        if not (isinstance(g, int) and g == 0):
                            e.tensor_copy(w_hi[:, par, r, :], w_raw[:, r, :]).then_inc(s_whi, 1)
                        wait_apart(e, s_passed, (s_whi, g * REP + r + 1))
                        e.tensor_tensor(w_lo[:, par, r, :], w_raw[:, r, :], w_hi[:, par, r, :].bitcast(F32),
                                        ALU.subtract).then_inc(s_wlo, 1)
                halve(0, 0)
                halve(1, 1)
                with e.Fori(1, HK // 2) as i:
                    for q in range(2):
                        halve(i * 2 + q, q)

            @block.scalar
            def _(e):
                e.wait_ge(s_w, 16)
                for r in range(REP):
                    e.activation(w_hi[:, 0, r, :], w_raw[:, r, :], ACT.Copy).then_inc(s_whi, 1)

                def step(i, j, u, live):
                    if live(0):
                        q = j % 2
                        wait(e, s_mm, u - 1)
                        e.wait_ge(s_o[q], (i * (PER // 2) + j // 2) * 16 + 16)
                        e.activation(o_hi[:, q, :, :], o_raw[:, q, :, :], ACT.Copy).then_inc(s_ohi, 1)

                turns(e, HK * CB, PER, 1, step)

            @block.vector
            def _(e):
                e.memset(att[:, :, :], 0.0).then_inc(s_acc, 1)

                def step(i, j, u, live):
                    if live(0):
                        q = j % 2
                        e.wait_ge(s_ohi, u + 1)
                        wait(e, s_mm, u - 1)
                        e.tensor_tensor(o_lo[:, q, :, :], o_raw[:, q, :, :], o_hi[:, q, :, :].bitcast(F32),
                                        ALU.subtract).then_inc(s_olo, 1)
                    if live(1):
                        m, jj = u - 1, j - 1
                        c, bank = jj % CB, (jj % 2) * KB
                        e.wait_ge(s_mm, m + 1)
                        wait(e, s_acc, m * KB + 1)
                        for ob in range(KB):
                            a = att[:, ob, c * 512:(c + 1) * 512]
                            e.tensor_tensor(a, a, ps[:, bank + ob, :], ALU.add).then_inc(s_acc, 1)

                turns(e, HK * CB, PER, 1, step)

            @block.tensor
            def _(e):
                def step(i, j, u, live):
                    if not live(0):
                        return
                    c, q, par, bank = j % CB, j % 2, (j // CB) % 2, (j % 2) * KB
                    if c == 0:
                        e.wait_ge(s_wlo, (i * 2 + j // CB + 1) * REP)
                    e.wait_ge(s_olo, u + 1)
                    wait(e, s_acc, (u - 1) * KB + 1)
                    for ob in range(KB):
                        for r in range(REP):
                            cols, x = slice(ob * P, (ob + 1) * P), slice(r * S, (r + 1) * S)
                            out = ps[:, bank + ob, :]
                            e.matmul(out, w_hi[:, par, r, cols], o_hi[:, q, :, x], start=(r == 0), stop=False)
                            e.matmul(out, w_hi[:, par, r, cols], o_lo[:, q, :, x], start=False, stop=False)
                            last = e.matmul(out, w_lo[:, par, r, cols], o_hi[:, q, :, x], start=False, stop=(r == REP - 1))
                    last.then_inc(s_mm, 1)

                turns(e, HK * CB, PER, 1, step)


def build(nc, dram, out_t):
    scratch = lambda n, shape: nc.dram_tensor(n, shape, F32).ap()
    taps = scratch("taps", [S, KPW])
    k_t = scratch("k_t", [PAGES * P, HK * PSIZE])
    x1_t = scratch("x1_t", [L, T])
    qk_t = scratch("qk_t", [B, P, NQU * P])
    v_own = scratch("v_own", [T, HK * D])
    o_t = scratch("o_t", [B, P, HK * P])
    with ExitStack() as ctx:
        ps = ctx.enter_context(nc.psum_tensor("ps", [P, 8, 512], F32))
        cst = ctx.enter_context(nc.sbuf_tensor("constants", [P, C_ALL], F32))
        with ExitStack() as first:
            sb = lambda c, n, s, d=F32: c.enter_context(nc.sbuf_tensor(n, s, d))
            ta, tb = (sb(first, n, [P, 2 * NT, D]) for n in ("ta", "tb"))
            cos, sin = (sb(first, n, [P, NT, D // 2]) for n in ("cos", "sin"))
            y_t = sb(first, "y_t", [P, KB, T])
            with ExitStack() as inputs:
                um = sb(inputs, "um", [P, KB, S, B])
                mrow = sb(inputs, "mrow", [P, KB, B])
                s4d_taps(nc, ps, dram, taps, cst, um, mrow, k_t)
                convolve(nc, ps, dram, taps, cst, um, mrow, y_t, cos, sin)
            xh, xl = (sb(first, n, [P, KB, T], F32R) for n in ("xh", "xl"))
            ffn(nc, ps, dram, ("w0", "b0", "g0", "a0", "lb0"), "0", y_t, dram["x_t"], x1_t, 1.0, cst,
                halves=(xh, xl), tables=(cos, sin, ta, tb))
            project(nc, ps, dram, cst, xh, xl, ta, tb, qk_t, v_own)
        attention(nc, ps, dram, cst, k_t, qk_t, v_own, o_t)
        with nc.sbuf_tensor("att", [P, KB, T], F32) as att:
            output_projection(nc, ps, dram, o_t, att)
            ffn(nc, ps, dram, ("w1", "b1", "g1", "a1", "lb1"), "1", att, x1_t, out_t, 2.0, cst)




def layouts(i):
    c = lambda a: np.ascontiguousarray(a)
    x = i["x"]
    out = {"cst": constants()}
    out["x_t"] = c(x.transpose(2, 0, 1).reshape(L, T))
    out["x_rev"] = c(x.transpose(2, 1, 0).reshape(KB, P, S, B)[:, ::-1].reshape(L, S, B))
    for n in ("itok_B_8_3872", "itok_Bx16_0_63", "itok_B_207_1644", "L0_cond_log_dt", "L0_cond_D",
              "L1_cond_q_norm_w", "L1_cond_k_norm_w"):
        out[n] = c(i[n])
    out["log_a"] = c(i["L0_cond_log_A_real"].reshape(HP, P).T)
    out["a_imag"] = c(i["L0_cond_A_imag"].reshape(HP, P).T)
    out["c"] = c(i["L0_cond_C"].reshape(HP, P, 2).transpose(1, 0, 2))
    w = np.concatenate([i["L1_cond_Wq"], i["L1_cond_Wk"], i["L1_cond_Wv"]])
    out["wqkv"] = c(w.reshape(NQU + HK // REP, 512, L).transpose(0, 2, 1))
    out["wo"] = c(i["L1_cond_Wo"].T.reshape(HQ, D, L))
    out["k_cache"] = c(i["L1_cond_k_cache"].reshape(PAGES * PSIZE, HK * D))
    out["v_cache"] = c(i["L1_cond_v_cache"].reshape(PAGES * PSIZE, HK * D))
    for n, p, g, a, b in (("0", "L0_ffn_", "W_gate", "A", "B"), ("1", "L1_ffn_", "W_router", "A_stack", "B_stack")):
        out["w" + n] = c(i[p + "W_base"].T)
        out["b" + n] = c(i[p + "b_base"].reshape(KB, P).T)
        out["g" + n] = c(i[p + g].T)
        out["a" + n] = c(i[p + a].reshape(E * R, L).T)
        out["lb" + n] = c(i[p + b].transpose(0, 2, 1).reshape(E * R, L))
    return out


def kernel(**inputs):
    import concourse.bacc as bacc
    from concourse.bass_utils import run_bass_kernel_spmd

    arrays = layouts({k: np.asarray(v) for k, v in inputs.items()})
    nc = bacc.Bacc("TRN2", target_bir_lowering=False, num_devices=1)
    dram = {k: nc.dram_tensor(k, v.shape, mybir.dt.from_np(v.dtype), kind="ExternalInput").ap() for k, v in arrays.items()}
    out_t = nc.dram_tensor("out_t", [L, T], F32, kind="ExternalOutput").ap()
    build(nc, dram, out_t)
    r = run_bass_kernel_spmd(nc, [arrays], core_ids=[0])
    return np.ascontiguousarray(r.results[0]["out_t"].reshape(L, B, S).transpose(1, 2, 0))
```
